# Optimizing a Trainium2 kernel written in Bass

```python
import numpy as np
import jax
import jax.numpy as jnp

def _softmax(x, axis=-1):
    return jax.nn.softmax(x, axis=axis)

def _gelu(x):
    return jax.nn.gelu(x, approximate=True)

def _silu(x):
    return jax.nn.silu(x)

def _sigmoid(x):
    return jax.nn.sigmoid(x)

def _layernorm(x, axis=-1, eps=1e-05):
    m = jnp.mean(x, axis=axis, keepdims=True)
    v = jnp.var(x, axis=axis, keepdims=True)
    return (x - m) / jnp.sqrt(v + eps)

def _scatter_add(tgt, idx, src, axis=0):
    return tgt.at[idx].add(src)

def _segment_sum(src, seg, n):
    return jax.ops.segment_sum(src, seg, n)
kernel_name = 'mk_audio_tower_d1_tok_audfeat768_r4_5dee88'

def setup_inputs(seed: int=0):
    np.random.seed(seed)
    _w = jnp.asarray

    def _rec_inputs():
        import jax
        import jax.numpy as jnp
        _rk = jax.random.key(seed)
        x = -0.000253961 + 1 * jax.random.normal(jax.random.fold_in(_rk, 1), (64, 90, 250), jnp.float32)
        return x
    x = _rec_inputs()

    def _L0_tok_setup():
        import jax, jax.numpy as jnp
        import numpy as np
        CHANNELS = 90
        PATCH = 16
        EMBED = 192
        key = jax.random.key(seed)
        k_x, k_w, k_b = jax.random.split(key, 3)
        in_feat = CHANNELS * PATCH
        x = jax.random.normal(k_x, (128, CHANNELS, 512), dtype=jnp.float32)
        bound = 1.0 / np.sqrt(in_feat)
        W = jax.random.uniform(k_w, (EMBED, in_feat), dtype=jnp.float32, minval=-bound, maxval=bound)
        b = jax.random.uniform(k_b, (EMBED,), dtype=jnp.float32, minval=-bound, maxval=bound)
        return {'x': x, 'W': W, 'b': b}
    _L0_tok_all = _L0_tok_setup()
    _L0_tok_in = {k: v for k, v in _L0_tok_all.items() if k in ('W', 'b')}
    del _L0_tok_all

    def _L0_attn_setup():
        import math
        import jax, jax.numpy as jnp
        import numpy as np
        B, N, D_IN, D_OUT = (8, 512, 192, 192)
        key = jax.random.key(seed)
        k1, k2, k3 = jax.random.split(key, 3)
        x = jax.random.normal(k1, (B, N, D_IN), dtype=jnp.float32)
        W_qkv = jax.random.normal(k2, (D_IN, 3 * D_OUT), dtype=jnp.float32) * (1.0 / math.sqrt(D_IN))
        b_qkv = jax.random.normal(k3, (3 * D_OUT,), dtype=jnp.float32) * 0.02
        return {'x': x, 'W_qkv': W_qkv, 'b_qkv': b_qkv}
    _L0_attn_all = _L0_attn_setup()
    _L0_attn_in = {k: v for k, v in _L0_attn_all.items() if k in ('W_qkv', 'b_qkv')}
    del _L0_attn_all

    def _L0_ffn_setup():
        import jax, jax.numpy as jnp
        import numpy as np
        E = 16
        K = 4
        H = 192
        I = 384
        LIMIT = 7.0
        ALPHA = 1.702
        EPS = 1e-05

        def rmsnorm(x, scale):
            xf = x.astype(jnp.float32)
            inv = jax.lax.rsqrt(jnp.mean(xf * xf, axis=-1, keepdims=True) + EPS)
            return (xf * inv).astype(x.dtype) * scale

        def swiglu(x, limit=LIMIT, alpha=ALPHA):
            x_glu = x[..., ::2]
            x_lin = x[..., 1::2]
            x_glu = jnp.minimum(x_glu, limit)
            x_lin = jnp.clip(x_lin, -limit, limit)
            return x_glu * jax.nn.sigmoid(alpha * x_glu) * (x_lin + 1.0)
        key = jax.random.key(seed)
        ks = jax.random.split(key, 7)
        s = 0.02
        return {'x': jax.random.normal(ks[0], (2, 256, H), dtype=jnp.float32), 'norm_scale': jnp.ones((H,), dtype=jnp.float32), 'gate_w': jax.random.normal(ks[1], (E, H), dtype=jnp.float32) * s, 'gate_b': jnp.zeros((E,), dtype=jnp.float32), 'mlp1_w': jax.random.normal(ks[2], (E, 2 * I, H), dtype=jnp.float32) * s, 'mlp1_b': jax.random.normal(ks[3], (E, 2 * I), dtype=jnp.float32) * s, 'mlp2_w': jax.random.normal(ks[4], (E, H, I), dtype=jnp.float32) * s, 'mlp2_b': jax.random.normal(ks[5], (E, H), dtype=jnp.float32) * s}
    _L0_ffn_all = _L0_ffn_setup()
    _L0_ffn_in = {k: v for k, v in _L0_ffn_all.items() if k in ('norm_scale', 'gate_w', 'gate_b', 'mlp1_w', 'mlp1_b', 'mlp2_w', 'mlp2_b')}
    del _L0_ffn_all
    return {'x': x, 'L0_tok_W': _L0_tok_in['W'], 'L0_tok_b': _L0_tok_in['b'], 'L0_attn_W_qkv': _L0_attn_in['W_qkv'], 'L0_attn_b_qkv': _L0_attn_in['b_qkv'], 'L0_ffn_norm_scale': _L0_ffn_in['norm_scale'], 'L0_ffn_gate_w': _L0_ffn_in['gate_w'], 'L0_ffn_gate_b': _L0_ffn_in['gate_b'], 'L0_ffn_mlp1_w': _L0_ffn_in['mlp1_w'], 'L0_ffn_mlp1_b': _L0_ffn_in['mlp1_b'], 'L0_ffn_mlp2_w': _L0_ffn_in['mlp2_w'], 'L0_ffn_mlp2_b': _L0_ffn_in['mlp2_b']}

def reference(x, L0_tok_W, L0_tok_b, L0_attn_W_qkv, L0_attn_b_qkv, L0_ffn_norm_scale, L0_ffn_gate_w, L0_ffn_gate_b, L0_ffn_mlp1_w, L0_ffn_mlp1_b, L0_ffn_mlp2_w, L0_ffn_mlp2_b):
    import jax
    import jax.numpy as jnp

    def _L0_tok_ref(x, W, b):
        import jax, jax.numpy as jnp
        import numpy as np
        CHANNELS = 90
        PATCH = 16
        EMBED = 192
        B, C, T = x.shape
        n = T // PATCH
        patches = x[:, :, :n * PATCH].reshape(B, C, n, PATCH)
        patches = patches.transpose(0, 2, 1, 3).reshape(B, n, C * PATCH)
        return jnp.einsum('bnf,ef->bne', patches, W) + b

    def _L0_attn_ref(x, W_qkv, b_qkv):
        import math
        import jax, jax.numpy as jnp
        import numpy as np
        B, N, D_IN, D_OUT = (8, 512, 192, 192)
        d_out = D_OUT
        qkv = jnp.einsum('bnd,de->bne', x, W_qkv) + b_qkv
        q = qkv[:, :, :d_out]
        k = qkv[:, :, d_out:2 * d_out]
        v = qkv[:, :, 2 * d_out:3 * d_out]
        scale = 1.0 / math.sqrt(d_out)
        scores = jnp.einsum('bqd,bkd->bqk', q, k) * scale
        attn = jax.nn.softmax(scores, axis=-1)
        context = jnp.einsum('bqk,bkd->bqd', attn, v)
        return context

    def _L0_ffn_ref(x, norm_scale, gate_w, gate_b, mlp1_w, mlp1_b, mlp2_w, mlp2_b):
        import jax, jax.numpy as jnp
        import numpy as np
        E = 16
        K = 4
        H = 192
        I = 384
        LIMIT = 7.0
        ALPHA = 1.702
        EPS = 1e-05

        def rmsnorm(x, scale):
            xf = x.astype(jnp.float32)
            inv = jax.lax.rsqrt(jnp.mean(xf * xf, axis=-1, keepdims=True) + EPS)
            return (xf * inv).astype(x.dtype) * scale

        def swiglu(x, limit=LIMIT, alpha=ALPHA):
            x_glu = x[..., ::2]
            x_lin = x[..., 1::2]
            x_glu = jnp.minimum(x_glu, limit)
            x_lin = jnp.clip(x_lin, -limit, limit)
            return x_glu * jax.nn.sigmoid(alpha * x_glu) * (x_lin + 1.0)
        B, T, _ = x.shape
        t = rmsnorm(x, norm_scale)
        g = jnp.einsum('bth,eh->bte', t, gate_w) + gate_b
        top_vals, top_idx = jax.lax.top_k(g, K)
        route_w = jax.nn.softmax(top_vals, axis=-1)
        t_flat = t.reshape(B * T, H)
        idx_flat = top_idx.reshape(B * T, K)
        w_flat = route_w.reshape(B * T, K)
        onehot = jax.nn.one_hot(idx_flat, E, dtype=t_flat.dtype)
        comb = jnp.einsum('nke,nk->ne', onehot, w_flat)
        h = jnp.einsum('nh,ech->nec', t_flat, mlp1_w) + mlp1_b
        a = swiglu(h)
        y = jnp.einsum('nec,ehc->neh', a, mlp2_w) + mlp2_b
        out_flat = jnp.einsum('neh,ne->nh', y, comb)
        return x + out_flat.reshape(B, T, H)
    h = _L0_tok_ref(x, L0_tok_W, L0_tok_b)
    h = h + _L0_attn_ref(_layernorm(h, axis=-1), L0_attn_W_qkv, L0_attn_b_qkv)
    h = h + _L0_ffn_ref(_layernorm(h, axis=-1), L0_ffn_norm_scale, L0_ffn_gate_w, L0_ffn_gate_b, L0_ffn_mlp1_w, L0_ffn_mlp1_b, L0_ffn_mlp2_w, L0_ffn_mlp2_b)
    return h

_drawn_inputs = setup_inputs


def setup_inputs(seed=0):
    import zlib

    import numpy as np

    out = dict(_drawn_inputs(seed))
    spreads = {'L0_ffn_norm_scale': (1.0, 0.6), 'L0_ffn_gate_b': (0.0, 0.71)}
    factors = {'L0_ffn_gate_w': 3.405,
     'L0_ffn_mlp1_w': 3.057,
     'L0_ffn_mlp1_b': 8.0,
     'L0_ffn_mlp2_w': 2.977,
     'L0_ffn_mlp2_b': 8.0}
    for name, (base, spread) in spreads.items():
        noise = np.random.default_rng([zlib.crc32(name.encode()), seed]).standard_normal(out[name].shape)
        drawn = base * np.exp(spread * noise) if base else spread * noise
        out[name] = jnp.asarray(drawn.astype(out[name].dtype))
    for name, factor in factors.items():
        out[name] = (out[name] * factor).astype(out[name].dtype)
    return out
```

```python
from contextlib import ExitStack

import concourse.bass as bass
from concourse import mybir

F32 = mybir.dt.float32
F16 = mybir.dt.float16
I32 = mybir.dt.int32
U32 = mybir.dt.uint32
ALU = mybir.AluOpType
ACT = mybir.ActivationFunctionType
AX = mybir.AxisListType

CLIPS, CHANNELS, PATCH, SEQ = 64, 90, 16, 15
TOKENS = CLIPS * SEQ
TILES = 8
TT = TOKENS // TILES
FEAT = CHANNELS * PATCH
FC = 12
FK = FEAT // FC
H = 192
HC = 2
HK = H // HC
E, K, I = 16, 4, 384
IC = I // 128
SLOTS = 128
MT = TOKENS * K // SLOTS + E - 1
PAIRS = TILES * K
EPS = 1e-5
LIMIT, ALPHA = 7.0, 1.702
SCALE = 1.0 / float(H) ** 0.5
OFF_CLIP = -1.0e30
SKIP = 1.0e6
W1E = HC * 2 * I
W2E = IC * H
RING = 3


def audio_tower_kernel(nc, x, tok_w, tok_b, qkv_w, qk_b, v_b, norm_scale, gate_w, gate_b,
                       w1, b1, w2, b2, out):
    ctx = ExitStack()
    with ctx:
        def sb(name, shape, dt=F32):
            return ctx.enter_context(nc.sbuf_tensor(name, shape, dt))

        def sem(name):
            return ctx.enter_context(nc.semaphore(name))

        t_rows = nc.dram_tensor("t_rows", (TOKENS, H), F32).ap()
        y_rows = nc.dram_tensor("y_rows", (TOKENS * K, H), F32).ap()

        w1_sb = sb("w1_sb", [HK + 1, E * W1E])
        w2_sb = sb("w2_sb", [128, E * W2E])
        tokw = sb("tokw", [128, FC * H])
        tokw_sb = tokw[0:FK, :].rearrange("p (c n) -> p c n", c=FC)
        qkvw = sb("qkvw", [128, HC * 3 * H])
        qkvw_sb = qkvw[0:HK, :].rearrange("p (c n) -> p c n", c=HC)
        gatew_sb = sb("gatew_sb", [HK, HC, E])
        b2_sb = sb("b2_sb", [E, H])
        tokb_sb = sb("tokb_sb", [TT, H])
        vb_sb = sb("vb_sb", [TT, H])
        qkb_sb = sb("qkb_sb", [HK, 4])
        nscale_sb = sb("nscale_sb", [TT, H])
        gateb_sb = sb("gateb_sb", [TT, E])
        ident = sb("ident", [128, 128])
        clip_mask = sb("clip_mask", [TT, TT])
        before = sb("before", [TT, SLOTS], F16)
        ones = sb("ones", [TT, SLOTS], F16)
        iota_e = sb("iota_e", [TT, E])
        iota_s = sb("iota_s", [TT, SLOTS], F16)
        iota_m = sb("iota_m", [128, MT])
        token_id = sb("token_id", [TT, TILES])
        choice1 = sb("choice1", [TT, K])
        lower = sb("lower", [128, E, E])
        eps_sb = sb("eps_sb", [TT, 1])
        x_sb = sb("x_sb", [FK, RING * FC * TT])
        h = sb("h", [TT, TILES, H])
        hn_all = sb("hn_all", [128, TILES * H])
        hn = hn_all[0:TT, :].rearrange("p (i n) -> p i n", i=TILES)
        ln2_all = sb("ln2_all", [128, TILES * H])
        ln2 = ln2_all[0:TT, :].rearrange("p (i n) -> p i n", i=TILES)
        bn = sb("bn", [TT, TILES, 6])
        mv = sb("mv", [TT, TILES, 2])
        std = sb("std", [TT, TILES])
        rstd = sb("rstd", [TT, TILES])
        rsq = sb("rsq", [TT, TILES])
        msq = sb("msq", [TT, TILES])
        rms = sb("rms", [TT, TILES])
        hT = sb("hT", [HK, 2, HC, TT])
        qk_all = sb("qk_all", [128, 2 * 4 * TT])
        qk = qk_all[0:HK, :].rearrange("p (b m t) -> p b m t", b=2, m=4)
        int_sb = qk_all[:, 0:3 * 128].bitcast(I32).rearrange("p (a n) -> p a n", a=3)
        v = sb("v", [TT, 2, H])
        sm = sb("sm", [TT, TT])
        nmax = sb("nmax", [TT, TILES])
        prob = sb("prob", [TT, TT])
        psums = sb("psums", [TT, TILES])
        rsum = sb("rsum", [TT, TILES])
        probT = sb("probT", [TT, TT])
        logits = sb("logits", [TT, TILES, E])
        top = sb("top", [TT, TILES, 8])
        topi = sb("topi", [TT, TILES, 8], U32)
        topif = sb("topif", [TT, TILES, K])
        nh = TILES * K * E
        hot = tokw[0:TT, 0:nh].rearrange("p (i k e) -> p i k e", i=TILES, k=K)
        prod = tokw[0:TT, nh:2 * nh].rearrange("p (i k e) -> p i k e", i=TILES, k=K)
        mask = sb("mask", [TT, TILES, E], F16)
        dv = sb("dv", [TT, TILES, K])
        ev = sb("ev", [TT, TILES, K])
        es = sb("es", [TT, TILES])
        route = sb("route", [TT, TILES, K])
        comb = sb("comb", [TT, TILES, E])
        combT = sb("combT", [E, TILES, TT])
        cnt_i = sb("cnt_i", [128, E], I32)
        cnt_t = sb("cnt_t", [128, E], I32)
        cnt = sb("cnt", [128, E])
        base_prod = qkvw[:, 0:E * E].rearrange("p (e f) -> p e f", e=E)
        base = sb("base", [128, E])
        base_end = sb("base_end", [128, E])
        base_s = sb("base_s", [128, E])
        pos_e = sb("pos_e", [TT, TILES, E])
        pos = sb("pos", [TT, PAIRS])
        pos_i = sb("pos_i", [TT, 3, PAIRS], I32)
        pos_f = sb("pos_f", [TT, 2, PAIRS])
        owner_cmp = qkvw[0:1, E * E:E * E + MT * E].rearrange("p (m e) -> p m e", m=MT)
        owner_f = sb("owner_f", [1, 2, MT])
        owner = sb("owner", [1, MT], I32)
        k1 = sb("k1", [SLOTS, MT])
        row4 = sb("row4", [SLOTS, 3, MT])
        get_row = sb("get_row", [SLOTS, MT], U32)
        put_row = sb("put_row", [SLOTS, MT], U32)
        xg = [hn_all[:, c * H:(c + 1) * H] for c in range(RING)]
        ysb = [hn_all[:, (RING + c) * H:(RING + c + 1) * H] for c in range(RING)]
        xT = sb("xT", [HK + 1, HC, SLOTS])
        glu, lin, sig, gs = (ln2_all[:, n * I:(n + 1) * I] for n in range(4))
        act_a = tokw[:, 2 * nh:2 * nh + I]
        aT = tokw[:, 2 * nh + I:2 * nh + 2 * I].rearrange("p (c t) -> p c t", c=IC)

        x_ring = x_sb[:, :].rearrange("p (r c t) -> p r c t", r=RING, c=FC)
        half = x_sb[:, :].bitcast(F16)
        nl = PAIRS * SLOTS
        nr = PAIRS * MT
        lo_hot = half[:, 0:nl].rearrange("p (c s) -> p c s", c=PAIRS)
        hi_hot = half[:, nl:nl + nr].rearrange("p (c m) -> p c m", c=PAIRS)
        hi_val = half[:, nl + nr:nl + 3 * nr].rearrange("p (c v m) -> p c v m", c=PAIRS, v=2)
        z = w2_sb[:, 0:TILES * K * H].rearrange("p (i n) -> p i n", i=TILES)

        bank = [ctx.enter_context(nc.psum_tensor(f"bank{n}", [128, 512], F32)) for n in range(8)]
        ps_emb = [bank[n][0:TT, 0:H] for n in (0, 1)]
        ps_hT = bank[2][0:HK, 0:HC * TT].rearrange("p (c t) -> p c t", c=HC)
        ps_qk = bank[3][0:HK, 0:4 * TT].rearrange("p (c t) -> p c t", c=4)
        ps_v = bank[4][0:TT, 0:H]
        ps_s = bank[5][0:TT, 0:TT]
        ps_pT = bank[6][0:TT, 0:TT]
        ps_o = bank[7][0:TT, 0:H]
        ps_tT = [bank[n][0:HK, 0:HC * TT].rearrange("p (c t) -> p c t", c=HC) for n in (0, 1)]
        ps_gate = [bank[n][0:TT, 0:TILES // 2 * E] for n in (2, 3)]
        ps_rank = bank[4][0:TT, 0:TILES * E]
        ps_cnt = bank[5][0:128, 0:E]
        ps_rows = bank[6][0:SLOTS, 0:2 * MT]
        ps_cT = [bank[n][0:E, 0:4 * TT].rearrange("p (c t) -> p c t", c=4) for n in (0, 1)]
        ps_b2 = [bank[n][0:TT, 0:2 * H].rearrange("p (c t) -> p c t", c=2) for n in (2, 3, 7, 5)]
        ps_glu = bank[0][:, 0:I]
        ps_lin = bank[1][:, 0:I]
        ps_aT = bank[2][:, 0:IC * SLOTS].rearrange("p (c t) -> p c t", c=IC)
        ps_xT = bank[3][0:HK, 0:HC * SLOTS].rearrange("p (c t) -> p c t", c=HC)
        ps_y = bank[4][:, 0:H]

        s_x = [sem(f"s_x{c}") for c in range(RING)]
        s_tokw = sem("s_tokw")
        s_small = sem("s_small")
        s_qkvw = sem("s_qkvw")
        s_w1 = sem("s_w1")
        s_w2 = sem("s_w2")
        N_SMALL = 7
        s_pool = sem("s_pool")
        s_const = sem("s_const")
        s_iotas = sem("s_iotas")
        s_emb = sem("s_emb")
        s_h = sem("s_h")
        s_stat = sem("s_stat")
        s_std = sem("s_std")
        s_hn = sem("s_hn")
        s_hT = sem("s_hT")
        s_hTc = sem("s_hTc")
        s_qk = sem("s_qk")
        s_v = sem("s_v")
        s_qkc = sem("s_qkc")
        s_vc = sem("s_vc")
        s_s = sem("s_s")
        s_sm = sem("s_sm")
        s_nmax = sem("s_nmax")
        s_prob = sem("s_prob")
        s_pT = sem("s_pT")
        s_pTc = sem("s_pTc")
        s_o = sem("s_o")
        s_h2 = sem("s_h2")
        s_stat2 = sem("s_stat2")
        s_std2 = sem("s_std2")
        s_msq = sem("s_msq")
        s_rms = sem("s_rms")
        s_ln2 = sem("s_ln2")
        s_t = sem("s_t")
        s_trow = sem("s_trow")
        s_tT = sem("s_tT")
        s_tTc = sem("s_tTc")
        s_gate = sem("s_gate")
        s_dve = sem("s_dve")
        s_mask = sem("s_mask")
        s_rank = sem("s_rank")
        s_dv = sem("s_dv")
        s_ev = sem("s_ev")
        s_comb = sem("s_comb")
        s_cT = sem("s_cT")
        s_cTc = sem("s_cTc")
        s_b2 = sem("s_b2")
        s_hot = sem("s_hot")
        s_rows = sem("s_rows")
        s_table = sem("s_table")
        s_base = sem("s_base")
        s_got = [sem(f"s_got{c}") for c in range(RING)]
        s_put = [sem(f"s_put{c}") for c in range(RING)]
        s_xT = sem("s_xT")
        s_xTc = sem("s_xTc")
        s_glu = sem("s_glu")
        s_gluc = sem("s_gluc")
        s_sig = sem("s_sig")
        s_lin = sem("s_lin")
        s_linc = sem("s_linc")
        s_gs = sem("s_gs")
        s_a = sem("s_a")
        s_aT = sem("s_aT")
        s_aTc = sem("s_aTc")
        s_y = sem("s_y")
        s_yc = sem("s_yc")
        s_z = [sem(f"s_z{i}") for i in range(TILES)]
        s_acc = sem("s_acc")
        s_out = sem("s_out")

        def wait(eng, s, value):
            if not isinstance(value, int) or value > 0:
                eng.wait_ge(s, value)

        def slot_steps(eng, step):
            for c in range(RING + 1):
                step(0, c)
            with eng.Fori(1, (MT - 1) // RING) as g:
                for c in range(1, RING + 1):
                    step(g, c)
            for c in range(1, (MT - 1) % RING + 1):
                step((MT - 1) // RING, c)

        block = ctx.enter_context(nc.Block())

        @block.sync
        def _(sp):
            sp.dma_start(tokw_sb[:, :, :], tok_w).then_inc(s_tokw, 16)
            for i in range(TILES):
                if i >= RING:
                    sp.wait_ge(s_emb, i - RING + 1)
                sp.dma_start(x_ring[:, i % RING], x[i]).then_inc(s_x[i % RING], 16)
                if i == 0:
                    sp.dma_start(tokb_sb[:, :], tok_b.broadcast_to([TT, H])).then_inc(s_small, 16)
                    sp.dma_start(vb_sb[:, :], v_b.broadcast_to([TT, H])).then_inc(s_small, 16)
                    sp.dma_start(nscale_sb[:, :], norm_scale.broadcast_to([TT, H])).then_inc(s_small, 16)
                    sp.dma_start(gateb_sb[:, :], gate_b.broadcast_to([TT, E])).then_inc(s_small, 16)
                    sp.dma_start(qkb_sb[:, :], qk_b).then_inc(s_small, 16)
                    sp.dma_start(gatew_sb[:, :, :], gate_w).then_inc(s_small, 16)
                    sp.dma_start(b2_sb[:, :], b2).then_inc(s_small, 16)
                if i == RING - 1:
                    sp.dma_start(qkvw_sb[:, :, :], qkv_w).then_inc(s_qkvw, 16)
            sp.dma_start(w1_sb[HK:HK + 1, :].rearrange("p (e c n) -> p e c n", e=E, c=HC)[:, :, HC - 1, :],
                         b1).then_inc(s_w1, 16)
            for e in range(E):
                sp.dma_start(w1_sb[0:HK, e * W1E:(e + 1) * W1E], w1[e]).then_inc(s_w1, 16)
                sp.dma_start(w2_sb[:, e * W2E:(e + 1) * W2E], w2[e]).then_inc(s_w2, 16)
            for i in range(TILES):
                sp.wait_ge(s_t, i + 1)
                sp.dma_start(t_rows[i * TT:(i + 1) * TT, :], hn[:, i, :]).then_inc(s_trow, 16)
            for c in range(RING):
                sp.wait_ge(s_put[c], 16 * (MT // RING))
            sp.wait_ge(s_y, MT)
            for i in range(TILES):
                sp.dma_start(z[0:TT, i, :],
                             y_rows[i * TT * K:(i + 1) * TT * K, :].rearrange("(t k) n -> t (k n)", k=K)
                             ).then_inc(s_z[i], 16)
            for i in range(TILES):
                sp.wait_ge(s_acc, i + 1)
                sp.dma_start(out[i * TT:(i + 1) * TT, :], h[:, i, :]).then_inc(s_out, 16)
            sp.wait_ge(s_out, 16 * TILES)

        @block.gpsimd
        def _(pool):
            n = 0

            def link(ins):
                nonlocal n
                n += 1
                ins.then_inc(s_pool, 1)
                pool.wait_ge(s_pool, n)

            g = nc.gpsimd
            g.memset(eps_sb[:, :], EPS).then_inc(s_const, 1)
            link(g.memset(ident[:, :], 0.0))
            g.affine_select(out=ident[:, :], in_=ident[:, :], compare_op=ALU.not_equal, fill=1.0, base=0,
                            pattern=[[-1, 128]], channel_multiplier=1).then_inc(s_const, 1)
            link(g.memset(clip_mask[:, :], 0.0))
            cm = clip_mask[:, :].rearrange("p (b w) -> p b w", w=SEQ)
            link(g.affine_select(out=cm, in_=cm, compare_op=ALU.is_ge, fill=OFF_CLIP, base=0,
                                 pattern=[[-SEQ, TT // SEQ], [0, SEQ]], channel_multiplier=1))
            g.affine_select(out=cm, in_=cm, compare_op=ALU.is_ge, fill=OFF_CLIP, base=SEQ - 1,
                            pattern=[[SEQ, TT // SEQ], [0, SEQ]], channel_multiplier=-1).then_inc(s_const, 1)
            g.memset(ones[:, :], 1.0).then_inc(s_const, 1)
            link(g.memset(before[:, :], 1.0))
            g.affine_select(out=before[:, :], in_=before[:, :], compare_op=ALU.is_ge, fill=0.0, base=-1,
                            pattern=[[1, SLOTS]], channel_multiplier=-1).then_inc(s_const, 1)
            link(g.memset(lower[:, :, :], 1.0))
            g.affine_select(out=lower[:, :, :], in_=lower[:, :, :], compare_op=ALU.is_ge, fill=0.0, base=-1,
                            pattern=[[1, E], [-1, E]], channel_multiplier=0).then_inc(s_const, 1)
            pool.wait_ge(s_const, 6)
            g.memset(xT[HK:HK + 1, :, :], 1.0).then_inc(s_const, 1)
            pool.wait_ge(s_const, 7)
            g.iota(int_sb[:, 0, :], pattern=[[1, 128]], base=0, channel_multiplier=0).then_inc(s_iotas, 1)
            g.iota(int_sb[:, 1, 0:TILES], pattern=[[TT, TILES]], base=0, channel_multiplier=1).then_inc(s_iotas, 1)
            g.iota(int_sb[:, 2, 0:K], pattern=[[1, K]], base=1, channel_multiplier=0).then_inc(s_iotas, 1)

            def gather(m, slot):
                g.indirect_dma_start(out=xg[slot], out_offset=None, in_=t_rows,
                                     in_offset=bass.IndirectOffsetOnAxis(ap=get_row[:, m:m + 1], axis=0),
                                     ).then_inc(s_got[slot], 16)

            def scatter(m, slot):
                g.indirect_dma_start(out=y_rows,
                                     out_offset=bass.IndirectOffsetOnAxis(ap=put_row[:, m:m + 1], axis=0),
                                     in_=ysb[slot], in_offset=None,
                                     bounds_check=TOKENS * K - 1, oob_is_err=False,
                                     ).then_inc(s_put[slot], 16)

            pool.wait_ge(s_table, 2)
            pool.wait_ge(s_trow, 16 * TILES)
            for m in range(2):
                gather(m, m)

            for j in range(MT):
                if j + 2 < MT:
                    if j > 0:
                        pool.wait_ge(s_xT, j)
                    gather(j + 2, (j + 2) % RING)
                if j > 0:
                    pool.wait_ge(s_yc, j)
                    scatter(j - 1, (j - 1) % RING)
            pool.wait_ge(s_yc, MT)
            scatter(MT - 1, (MT - 1) % RING)

        @block.scalar
        def _(act):
            a = nc.scalar
            act.wait_ge(s_const, 1)

            def roots(dst, src, hf, done):
                t = slice(4 * hf, 4 * hf + 4)
                a.activation(dst[:, t], src, ACT.Sqrt, bias=eps_sb[:, 0:1]).then_inc(done, 1)

            def copy_hT(i):
                act.wait_ge(s_hT, i + 1)
                if i >= 2:
                    act.wait_ge(s_v, i - 1)
                a.copy(hT[:, i % 2], ps_hT).then_inc(s_hTc, 1)

            def softmax(i):
                act.wait_ge(s_nmax, i + 1)
                if i >= 1:
                    act.wait_ge(s_pT, i)
                a.activation(prob[:, :], sm[:, :], ACT.Exp, bias=nmax[:, i:i + 1],
                             accum_out=psums[:, i:i + 1]).then_inc(s_prob, 1)

            def copy_pT(i):
                act.wait_ge(s_pT, i + 1)
                if i >= 1:
                    act.wait_ge(s_o, i)
                a.copy(probT[:, :], ps_pT).then_inc(s_pTc, 1)

            def roots2(hf):
                act.wait_ge(s_stat2, 4 * hf + 4)
                roots(std, mv[:, 4 * hf:4 * hf + 4, 1], hf, s_std2)
                act.wait_ge(s_msq, hf + 1)
                roots(rms, msq[:, 4 * hf:4 * hf + 4], hf, s_rms)

            for hf in range(2):
                act.wait_ge(s_stat, 4 * hf + 4)
                roots(std, mv[:, 4 * hf:4 * hf + 4, 1], hf, s_std)
            copy_hT(0)
            for i in range(TILES + 1):
                if i >= 1:
                    softmax(i - 1)
                    copy_pT(i - 1)
                if i + 1 < TILES:
                    copy_hT(i + 1)
                if i == 5:
                    roots2(0)
            roots2(1)
            for i in range(TILES):
                act.wait_ge(s_tT, i + 1)
                if i >= 2:
                    act.wait_ge(s_gate, i - 1)
                a.copy(hT[:, i % 2], ps_tT[i % 2]).then_inc(s_tTc, 1)
            act.wait_ge(s_dv, 1)
            a.activation(ev[:, :, :], dv[:, :, :], ACT.Exp).then_inc(s_ev, 1)
            for n in range(2):
                act.wait_ge(s_cT, n + 1)
                a.copy(combT[:, 4 * n:4 * n + 4, :], ps_cT[n]).then_inc(s_cTc, 1)

            def copy_xT(j):
                act.wait_ge(s_xT, j + 1)
                wait(act, s_lin, j)
                a.copy(xT[0:HK, :, :], ps_xT).then_inc(s_xTc, 1)

            def copy_aT(j):
                act.wait_ge(s_aT, j + 1)
                wait(act, s_y, j)
                a.copy(aT[:, :, :], ps_aT).then_inc(s_aTc, 1)

            def copy_y(j, slot, uses):
                act.wait_ge(s_y, j + 1)
                wait(act, s_put[slot], 16 * uses)
                a.copy(ysb[slot], ps_y).then_inc(s_yc, 1)

            copy_xT(0)

            def step(gi, c):
                j = RING * gi + c
                first = isinstance(j, int) and j == 0
                if not first:
                    copy_aT(j - 1)
                act.wait_ge(s_gluc, j + 1)
                wait(act, s_gs, j)
                a.activation(sig, glu, ACT.Sigmoid, scale=ALPHA).then_inc(s_sig, 1)
                if not (isinstance(j, int) and j == MT - 1):
                    copy_xT(j + 1)
                if not first:
                    copy_y(j - 1, (c - 1) % RING, gi + (c - 1) // RING)

            slot_steps(act, step)
            copy_aT(MT - 1)
            copy_y(MT - 1, (MT - 1) % RING, (MT - 1) // RING)

        @block.vector
        def _(dve):
            d = nc.vector
            n = 0

            def link(ins):
                nonlocal n
                n += 1
                ins.then_inc(s_dve, 1)
                dve.wait_ge(s_dve, n)

            def stats(i, done):
                link(d.bn_stats(bn[:, i, :], h[:, i, :]))
                d.bn_aggr(mv[:, i, :], bn[:, i, :]).then_inc(done, 1)

            dve.wait_ge(s_iotas, 3)
            d.tensor_copy(iota_e[:, :], int_sb[0:TT, 0, 0:E])
            d.tensor_copy(iota_s[:, :], int_sb[0:TT, 0, 0:SLOTS])
            d.tensor_copy(iota_m[:, :], int_sb[:, 0, 0:MT])
            d.tensor_copy(token_id[:, :], int_sb[0:TT, 1, 0:TILES])
            link(d.tensor_copy(choice1[:, :], int_sb[0:TT, 2, 0:K]))

            dve.wait_ge(s_small, 16 * N_SMALL)

            def normalise(hf):
                dve.wait_ge(s_std, hf + 1)
                t = slice(4 * hf, 4 * hf + 4)
                link(d.reciprocal(rstd[:, t], std[:, t]))
                for i in range(4 * hf, 4 * hf + 4):
                    d.tensor_scalar(hn[:, i, :], h[:, i, :], mv[:, i, 0:1], rstd[:, i:i + 1],
                                    ALU.subtract, ALU.mult).then_inc(s_hn, 1)

            for i in range(TILES):
                dve.wait_ge(s_emb, i + 1)
                d.tensor_tensor(h[:, i, :], ps_emb[i % 2], tokb_sb[:, :], ALU.add).then_inc(s_h, 1)
                dve.wait_ge(s_h, i + 1)
                stats(i, s_stat)
                if i == 4:
                    normalise(0)
            normalise(1)

            def scores(i):
                dve.wait_ge(s_s, i + 1)
                if i >= 1:
                    dve.wait_ge(s_prob, i)
                d.scalar_tensor_tensor(out=sm[:, :], in0=ps_s, scalar=SCALE, in1=clip_mask[:, :],
                                       op0=ALU.mult, op1=ALU.add).then_inc(s_sm, 1)
                dve.wait_ge(s_sm, i + 1)
                d.tensor_reduce(nmax[:, i:i + 1], sm[:, :], AX.X, ALU.max, negate=True).then_inc(s_nmax, 1)

            def copy_qkv(i):
                dve.wait_ge(s_qk, i + 1)
                if i >= 2:
                    dve.wait_ge(s_o, i - 1)
                d.tensor_tensor(qk[:, i % 2], ps_qk, qkb_sb[:, :].unsqueeze(2).to_broadcast([HK, 4, TT]),
                                ALU.add).then_inc(s_qkc, 1)
                dve.wait_ge(s_v, i + 1)
                d.tensor_tensor(v[:, i % 2, :], ps_v, vb_sb[:, :], ALU.add).then_inc(s_vc, 1)

            def residual(i):
                dve.wait_ge(s_prob, i + 1)
                link(d.reciprocal(rsum[:, i:i + 1], psums[:, i:i + 1]))
                dve.wait_ge(s_o, i + 1)
                d.scalar_tensor_tensor(out=h[:, i, :], in0=ps_o, scalar=rsum[:, i:i + 1], in1=h[:, i, :],
                                       op0=ALU.mult, op1=ALU.add).then_inc(s_h2, 1)
                dve.wait_ge(s_h2, i + 1)
                stats(i, s_stat2)

            def normalise2(hf):
                t = slice(4 * hf, 4 * hf + 4)
                dve.wait_ge(s_std2, hf + 1)
                link(d.reciprocal(rstd[:, t], std[:, t]))
                link(d.tensor_tensor(rsq[:, t], rstd[:, t], rstd[:, t], ALU.mult))
                d.tensor_tensor(msq[:, t], rsq[:, t], mv[:, t, 1], ALU.mult).then_inc(s_msq, 1)
                for i in range(4 * hf, 4 * hf + 4):
                    d.tensor_scalar(ln2[:, i, :], h[:, i, :], mv[:, i, 0:1], rstd[:, i:i + 1],
                                    ALU.subtract, ALU.mult).then_inc(s_ln2, 1)
                dve.wait_ge(s_rms, hf + 1)
                dve.wait_ge(s_ln2, 4 * hf + 4)
                link(d.reciprocal(rsq[:, t], rms[:, t]))
                for i in range(4 * hf, 4 * hf + 4):
                    d.scalar_tensor_tensor(out=hn[:, i, :], in0=ln2[:, i, :], scalar=rsq[:, i:i + 1],
                                           in1=nscale_sb[:, :], op0=ALU.mult, op1=ALU.mult).then_inc(s_t, 1)

            dve.wait_ge(s_const, 3)
            for i in range(TILES + 1):
                if i >= 1:
                    scores(i - 1)
                if i < TILES:
                    copy_qkv(i)
                if i >= 1:
                    residual(i - 1)
                if i == 5:
                    normalise2(0)
            normalise2(1)
            d.tensor_tensor(h[:, :, :], h[:, :, :], ln2[:, :, :], ALU.add).then_inc(s_base, 1)

            for hf in range(2):
                t = slice(4 * hf, 4 * hf + 4)
                dve.wait_ge(s_gate, 4 * hf + 4)
                link(d.tensor_tensor(logits[:, t, :], ps_gate[hf].rearrange("p (i e) -> p i e", e=E),
                                     gateb_sb[:, :].unsqueeze(1).to_broadcast([TT, 4, E]), ALU.add))
                for i in range(4 * hf, 4 * hf + 4):
                    ins = d.max(top[:, i, :], logits[:, i, :])
                    if i % 4 == 3:
                        link(ins)
                for i in range(4 * hf, 4 * hf + 4):
                    ins = d.max_index(topi[:, i, :], top[:, i, :], logits[:, i, :])
                    if i % 4 == 3:
                        link(ins)
            d.tensor_tensor(dv[:, :, :], top[:, :, 0:K], top[:, :, 0:1].to_broadcast([TT, TILES, K]),
                            ALU.subtract).then_inc(s_dv, 1)
            link(d.tensor_copy(topif[:, :, :], topi[:, :, 0:K]))
            hot3 = tokw[0:TT, 0:nh].rearrange("p (c e) -> p c e", e=E)
            prod3 = tokw[0:TT, nh:2 * nh].rearrange("p (c e) -> p c e", e=E)
            link(d.tensor_tensor(hot3, topif[:, :, :].rearrange("p i k -> p (i k)").unsqueeze(2)
                                 .to_broadcast([TT, PAIRS, E]),
                                 iota_e[:, :].unsqueeze(1).to_broadcast([TT, PAIRS, E]), ALU.is_equal))
            with nc.allow_low_precision("counts of 0 and 1 are exact"):
                d.tensor_reduce(mask[:, :, :], hot[:, :, :, :].rearrange("p i k e -> p i e k"), AX.X,
                                ALU.add).then_inc(s_mask, 1)
            dve.wait_ge(s_ev, 1)
            link(d.tensor_reduce(es[:, :], ev[:, :, :], AX.X, ALU.add))
            link(d.reciprocal(es[:, :], es[:, :]))
            link(d.tensor_tensor(route[:, :, :], ev[:, :, :], es[:, :].unsqueeze(2).to_broadcast([TT, TILES, K]),
                                 ALU.mult))
            dve.wait_ge(s_rank, 2)
            link(d.tensor_scalar(cnt_i[:, :], ps_cnt, float(SLOTS - 1), None, ALU.add))
            link(d.tensor_scalar(cnt_t[:, :], cnt_i[:, :], 7, None, ALU.arith_shift_right))
            link(d.tensor_copy(cnt[:, :], cnt_t[:, :]))
            link(d.tensor_tensor(base_prod[:, :, :], lower[:, :, :],
                                 cnt[:, :].unsqueeze(1).to_broadcast([128, E, E]), ALU.mult))
            link(d.tensor_reduce(base[:, :], base_prod[:, :, :], AX.X, ALU.add))
            d.tensor_tensor(base_end[:, :], base[:, :], cnt[:, :], ALU.add)
            link(d.tensor_scalar(base_s[:, :], base[:, :], float(SLOTS), None, ALU.mult))
            link(d.tensor_tensor(pos_e[:, :, :], ps_rank.rearrange("p (i e) -> p i e", e=E),
                                 base_s[0:TT, :].unsqueeze(1).to_broadcast([TT, TILES, E]), ALU.add))
            for k in range(K):
                ins = d.tensor_tensor(prod[:, :, k, :], hot[:, :, k, :], pos_e[:, :, :], ALU.mult)
            link(ins)
            link(d.tensor_reduce(pos[:, :], prod3, AX.X, ALU.add))
            link(d.tensor_copy(pos_i[:, 0, :], pos[:, :]))
            d.tensor_scalar(pos_i[:, 1, :], pos_i[:, 0, :], SLOTS - 1, None, ALU.bitwise_and)
            link(d.tensor_scalar(pos_i[:, 2, :], pos_i[:, 0, :], 7, None, ALU.arith_shift_right))
            link(d.tensor_copy(pos_f[:, :, :], pos_i[:, 1:3, :]))
            link(d.tensor_tensor(hi_hot, pos_f[:, 1, :].unsqueeze(2).to_broadcast([TT, PAIRS, MT]),
                                 iota_m[0:TT, :].unsqueeze(1).to_broadcast([TT, PAIRS, MT]), ALU.is_equal))
            for i in range(TILES):
                d.tensor_scalar(hi_val[:, K * i:K * i + K, 0, :], hi_hot[:, K * i:K * i + K, :],
                                token_id[:, i:i + 1], None, ALU.mult)
            for k in range(K):
                d.tensor_scalar(hi_val[:, k::K, 1, :], hi_hot[:, k::K, :], choice1[:, k:k + 1], None, ALU.mult)
            for c in range(PAIRS):
                d.tensor_scalar(lo_hot[:, c, :], iota_s[:, :], pos_f[:, 0, c:c + 1], None,
                                ALU.is_equal).then_inc(s_hot, 1)
            d.tensor_tensor(owner_cmp[:, :, :], base_end[0:1, :].unsqueeze(1).to_broadcast([1, MT, E]),
                            iota_m[0:1, :].unsqueeze(2).to_broadcast([1, MT, E]), ALU.is_le)
            for i in range(TILES):
                for_k = prod[:, i, :, :].rearrange("p k e -> p e k")
                d.tensor_tensor(for_k, hot[:, i, :, :].rearrange("p k e -> p e k"),
                                route[:, i, :].unsqueeze(1).to_broadcast([TT, E, K]), ALU.mult)
            link(d.tensor_scalar(k1[:, 0:1], iota_m[:, 0:1], 0.0, None, ALU.mult))
            d.tensor_reduce(owner_f[:, 0, :], owner_cmp[:, :, :], AX.X, ALU.add)
            link(d.tensor_reduce(comb[:, :, :], prod[:, :, :, :].rearrange("p i k e -> p i e k"), AX.X, ALU.add))
            d.tensor_scalar(owner[:, :], owner_f[:, 0, :], float(E - 1), None, ALU.min).then_inc(s_comb, 1)
            dve.wait_ge(s_rows, 1)
            d.tensor_copy(get_row[:, :], ps_rows[:, 0:MT]).then_inc(s_table, 1)
            link(d.tensor_copy(k1[:, :], ps_rows[:, MT:2 * MT]))
            d.scalar_tensor_tensor(out=row4[:, 0, :], in0=ps_rows[:, 0:MT], scalar=float(K), in1=k1[:, :],
                                   op0=ALU.mult, op1=ALU.add)
            link(d.tensor_scalar(row4[:, 1, :], k1[:, :], 0.0, SKIP + 1.0, ALU.is_equal, ALU.mult))
            link(d.tensor_tensor(row4[:, 2, :], row4[:, 0, :], row4[:, 1, :], ALU.add))
            d.tensor_scalar(put_row[:, :], row4[:, 2, :], -1.0, None, ALU.add).then_inc(s_table, 1)
            for q in range(4):
                dve.wait_ge(s_b2, q + 1)
                if q == 0:
                    dve.wait_ge(s_base, 1)
                d.tensor_tensor(h[:, 2 * q:2 * q + 2, :], h[:, 2 * q:2 * q + 2, :], ps_b2[q],
                                ALU.add).then_inc(s_base, 1)

            def step(gi, c):
                j = RING * gi + c
                dve.wait_ge(s_glu, j + 1)
                wait(dve, s_gs, j)
                d.tensor_scalar(glu, ps_glu, LIMIT, None, ALU.min).then_inc(s_gluc, 1)
                dve.wait_ge(s_sig, j + 1)
                wait(dve, s_a, j)
                d.tensor_tensor(gs, glu, sig, ALU.mult).then_inc(s_gs, 1)
                dve.wait_ge(s_lin, j + 1)
                d.tensor_scalar(lin, ps_lin, LIMIT, -LIMIT, ALU.min, ALU.max).then_inc(s_linc, 1)
                dve.wait_ge(s_linc, j + 1)
                dve.wait_ge(s_gs, j + 1)
                wait(dve, s_aT, j)
                d.scalar_tensor_tensor(out=act_a, in0=lin, scalar=1.0, in1=gs,
                                       op0=ALU.add, op1=ALU.mult).then_inc(s_a, 1)

            slot_steps(dve, step)

            dve.wait_ge(s_base, 5)
            for i in range(TILES):
                dve.wait_ge(s_z[i], 16)
                for k in range(K):
                    ins = d.scalar_tensor_tensor(out=h[:, i, :], in0=z[0:TT, i, k * H:(k + 1) * H],
                                                 scalar=route[:, i, k:k + 1], in1=h[:, i, :],
                                                 op0=ALU.mult, op1=ALU.add)
                    if k < K - 1:
                        link(ins)
                ins.then_inc(s_acc, 1)

        @block.tensor
        def _(pe):
            t = nc.tensor

            pe.wait_ge(s_tokw, 16)
            for i in range(TILES):
                pe.wait_ge(s_x[i % RING], 16 * (i // RING + 1))
                if i >= 2:
                    pe.wait_ge(s_h, i - 1)
                for c in range(FC):
                    ins = t.matmul(ps_emb[i % 2], x_ring[:, i % RING, c, :], tokw_sb[:, c, :],
                                   start=(c == 0), stop=(c == FC - 1))
                ins.then_inc(s_emb, 1)

            pe.wait_ge(s_const, 7)
            pe.wait_ge(s_qkvw, 16)

            def turn_h(i):
                pe.wait_ge(s_hn, i + 1)
                if i >= 1:
                    pe.wait_ge(s_hTc, i)
                for c in range(HC):
                    ins = t.transpose(ps_hT[:, c, :], hn[:, i, c * HK:(c + 1) * HK], ident[0:TT, 0:TT])
                ins.then_inc(s_hT, 1)

            def qkv(i):
                pe.wait_ge(s_hTc, i + 1)
                if i >= 1:
                    pe.wait_ge(s_vc, i)
                for m in range(4):
                    for c in range(HC):
                        ins = t.matmul(ps_qk[:, m, :], qkvw_sb[:, c, m * HK:(m + 1) * HK], hT[:, i % 2, c, :],
                                       start=(c == 0), stop=(c == HC - 1))
                ins.then_inc(s_qk, 1)
                for c in range(HC):
                    ins = t.matmul(ps_v, hT[:, i % 2, c, :], qkvw_sb[:, c, 2 * H:3 * H],
                                   start=(c == 0), stop=(c == HC - 1))
                ins.then_inc(s_v, 1)

            def score(i):
                pe.wait_ge(s_qkc, i + 1)
                if i >= 1:
                    pe.wait_ge(s_sm, i)
                for c in range(HC):
                    ins = t.matmul(ps_s, qk[:, i % 2, c, :], qk[:, i % 2, HC + c, :],
                                   start=(c == 0), stop=(c == HC - 1))
                ins.then_inc(s_s, 1)

            def turn_p(i):
                pe.wait_ge(s_prob, i + 1)
                if i >= 1:
                    pe.wait_ge(s_pTc, i)
                t.transpose(ps_pT, prob[:, :], ident[0:TT, 0:TT]).then_inc(s_pT, 1)

            def context(i):
                pe.wait_ge(s_pTc, i + 1)
                pe.wait_ge(s_vc, i + 1)
                if i >= 1:
                    pe.wait_ge(s_h2, i)
                t.matmul(ps_o, probT[:, :], v[:, i % 2, :], start=True, stop=True).then_inc(s_o, 1)

            turn_h(0)
            for i in range(TILES + 1):
                if i >= 1:
                    score(i - 1)
                if i < TILES:
                    qkv(i)
                if i >= 1:
                    turn_p(i - 1)
                if i + 1 < TILES:
                    turn_h(i + 1)
                if i >= 1:
                    context(i - 1)

            pe.wait_ge(s_small, 16 * N_SMALL)

            def turn_t(i):
                pe.wait_ge(s_t, i + 1)
                if i >= 2:
                    pe.wait_ge(s_tTc, i - 1)
                for c in range(HC):
                    ins = t.transpose(ps_tT[i % 2][:, c, :], hn[:, i, c * HK:(c + 1) * HK], ident[0:TT, 0:TT])
                ins.then_inc(s_tT, 1)

            def gate(i):
                pe.wait_ge(s_tTc, i + 1)
                if i == 4:
                    pe.wait_ge(s_qkc, TILES)
                for c in range(HC):
                    ins = t.matmul(ps_gate[i // 4][:, i % 4 * E:(i % 4 + 1) * E], hT[:, i % 2, c, :],
                                   gatew_sb[:, c, :], start=(c == 0), stop=(c == HC - 1))
                ins.then_inc(s_gate, 1)

            turn_t(0)
            for i in range(TILES):
                if i + 1 < TILES:
                    turn_t(i + 1)
                gate(i)

            pe.wait_ge(s_mask, 1)
            m2 = mask[:, :, :].rearrange("p i e -> p (i e)")
            ins = t.matmul(ps_rank, before[:, 0:TT], m2, start=True, stop=False)
            for s in range(1, TILES):
                ins = t.matmul(ps_rank[:, s * E:TILES * E], ones[:, 0:TT], m2[:, 0:(TILES - s) * E],
                               start=False, stop=(s == TILES - 1))
            ins.then_inc(s_rank, 1)
            for i in range(TILES):
                ins = t.matmul(ps_cnt, ones[:, :], mask[:, i, :], start=(i == 0), stop=(i == TILES - 1))
            ins.then_inc(s_rank, 1)
            for c in range(PAIRS):
                pe.wait_ge(s_hot, c + 1)
                ins = t.matmul(ps_rows, lo_hot[:, c, :], hi_val[:, c, :, :],
                               start=(c == 0), stop=(c == PAIRS - 1))
            ins.then_inc(s_rows, 1)
            pe.wait_ge(s_comb, 1)
            for n in range(2):
                for i in range(4):
                    ins = t.transpose(ps_cT[n][:, i, :], comb[:, 4 * n + i, :], ident[0:TT, 0:TT])
                ins.then_inc(s_cT, 1)
            for q in range(4):
                pe.wait_ge(s_cTc, q // 2 + 1)
                for i in range(2):
                    ins = t.matmul(ps_b2[q][:, i, :], combT[:, 2 * q + i, :], b2_sb[:, :],
                                   start=True, stop=True)
                ins.then_inc(s_b2, 1)

            pe.wait_ge(s_w1, 16 * (E + 1))
            pe.wait_ge(s_w2, 16 * E)
            pe.wait_ge(s_base, 5)

            def turn_x(slot, uses):
                pe.wait_ge(s_got[slot], 16 * uses)
                for c in range(HC):
                    ins = t.transpose(ps_xT[:, c, :], xg[slot][:, c * HK:(c + 1) * HK], ident[:, :])
                ins.then_inc(s_xT, 1)

            def expert(j):
                return pe.value_load(owner[0:1, bass.ds(j, 1) if not isinstance(j, int) else slice(j, j + 1)],
                                     min_val=0, max_val=E - 1)

            def up(e, part, dst):
                for c in range(HC):
                    rows = HK + (c == HC - 1)
                    ins = t.matmul(dst, xT[0:rows, c, :],
                                   w1_sb[0:rows, bass.ds(e * W1E + (2 * c + part) * I, I)],
                                   start=(c == 0), stop=(c == HC - 1))
                return ins

            def turn_a(j):
                pe.wait_ge(s_a, j + 1)
                wait(pe, s_aTc, j)
                for c in range(IC):
                    ins = t.transpose(ps_aT[:, c, :], act_a[:, c * 128:(c + 1) * 128], ident[:, :])
                ins.then_inc(s_aT, 1)

            def down(e, j):
                pe.wait_ge(s_aTc, j + 1)
                wait(pe, s_yc, j)
                for c in range(IC):
                    ins = t.matmul(ps_y, aT[:, c, :], w2_sb[:, bass.ds(e * W2E + c * H, H)],
                                   start=(c == 0), stop=(c == IC - 1))
                ins.then_inc(s_y, 1)

            def step(gi, c):
                j = RING * gi + c
                first = isinstance(j, int) and j == 0
                last = isinstance(j, int) and j == MT - 1
                e = expert(j)
                pe.wait_ge(s_xTc, j + 1)
                wait(pe, s_gluc, j)
                up(e, 0, ps_glu).then_inc(s_glu, 1)
                if not first:
                    turn_a(j - 1)
                wait(pe, s_linc, j)
                up(e, 1, ps_lin).then_inc(s_lin, 1)
                if not last:
                    pe.wait_ge(s_xTc, j + 1)
                    turn_x((c + 1) % RING, gi + (c + 1) // RING + 1)
                if not first:
                    down(expert(j - 1), j - 1)

            turn_x(0, 1)
            slot_steps(pe, step)
            turn_a(MT - 1)
            down(expert(MT - 1), MT - 1)


def kernel(**inputs):
    import numpy as np
    import concourse.bacc as bacc
    from concourse.bass_utils import run_bass_kernel_spmd

    a = {k: np.asarray(v) for k, v in inputs.items()}
    x = a["x"][:, :, :SEQ * PATCH].reshape(TILES, CLIPS // TILES, CHANNELS, SEQ, PATCH)
    x = x.transpose(0, 2, 4, 1, 3).reshape(TILES, FC, FK, TT).transpose(0, 2, 1, 3)
    w1 = a["L0_ffn_mlp1_w"].reshape(E, I, 2, HC, HK).transpose(0, 4, 3, 2, 1).reshape(E, HK, W1E)
    b1 = a["L0_ffn_mlp1_b"].reshape(E, I, 2).transpose(0, 2, 1).reshape(1, E, 2 * I)
    w2 = a["L0_ffn_mlp2_w"].reshape(E, H, IC, 128).transpose(0, 3, 2, 1).reshape(E, 128, W2E)
    arrays = {
        "x": x,
        "tok_w": a["L0_tok_W"].reshape(H, FC, FK).transpose(2, 1, 0),
        "tok_b": a["L0_tok_b"].reshape(1, H),
        "qkv_w": a["L0_attn_W_qkv"].reshape(HC, HK, 3 * H).transpose(1, 0, 2),
        "qk_b": a["L0_attn_b_qkv"][:2 * H].reshape(4, HK).transpose(1, 0),
        "v_b": a["L0_attn_b_qkv"][2 * H:].reshape(1, H),
        "norm_scale": a["L0_ffn_norm_scale"].reshape(1, H),
        "gate_w": a["L0_ffn_gate_w"].reshape(E, HC, HK).transpose(2, 1, 0),
        "gate_b": a["L0_ffn_gate_b"].reshape(1, E),
        "w1": w1,
        "b1": b1,
        "w2": w2,
        "b2": a["L0_ffn_mlp2_b"],
    }
    arrays = {f"in_{k}": np.ascontiguousarray(v) for k, v in arrays.items()}
    nc = bacc.Bacc("TRN2", target_bir_lowering=False, num_devices=1)
    args = [nc.dram_tensor(k, v.shape, mybir.dt.from_np(v.dtype), kind="ExternalInput").ap()
            for k, v in arrays.items()]
    out = nc.dram_tensor("out", (TOKENS, H), F32, kind="ExternalOutput").ap()
    audio_tower_kernel(nc, *args, out)
    r = run_bass_kernel_spmd(nc, [arrays], core_ids=[0])
    return r.results[0]["out"].reshape(CLIPS, SEQ, H)
```

```python
from contextlib import ExitStack

import concourse.bass as bass
from concourse import mybir

F32 = mybir.dt.float32
F16 = mybir.dt.float16
I32 = mybir.dt.int32
U32 = mybir.dt.uint32
ALU = mybir.AluOpType
ACT = mybir.ActivationFunctionType
AX = mybir.AxisListType

CLIPS, CHANNELS, PATCH, SEQ = 64, 90, 16, 15
TOKENS = CLIPS * SEQ
TILES = 8
TT = TOKENS // TILES
FEAT = CHANNELS * PATCH
FC = 12
FK = FEAT // FC
H = 192
HC = 2
HK = H // HC
E, K, I = 16, 4, 384
IC = I // 128
SLOTS = 128
SLOT_BITS = 7
MT = TOKENS * K // SLOTS + E - 1
PAIRS = TILES * K
AHEAD = 2
EPS = 1e-5
LIMIT, ALPHA = 7.0, 1.702
SCALE = 1.0 / float(H) ** 0.5
OFF_CLIP = -1.0e30
ROW = H + E
W1E = HC * 2 * I
W2E = IC * H
RING = 3
FIRST = 3
POOL_HOTS = 9


def audio_tower_kernel(nc, x, tok_w, tok_b, qkv_w, qk_b, v_b, norm_scale, gate_w, gate_b,
                       w1, b1, w2, b2, out):
    ctx = ExitStack()
    with ctx:
        def sb(name, shape, dt=F32):
            return ctx.enter_context(nc.sbuf_tensor(name, shape, dt))

        def sem(name):
            return ctx.enter_context(nc.semaphore(name))

        t_rows = nc.dram_tensor("t_rows", (TOKENS, ROW), F32).ap()

        w1_sb = sb("w1_sb", [128, E * W1E])
        w2_sb = sb("w2_sb", [128, E * W2E])
        tokw = sb("tokw", [128, FC * H])
        tokw_sb = tokw[0:FK, :].rearrange("p (c n) -> p c n", c=FC)
        qkvw = sb("qkvw", [128, HC * 3 * H])
        qkvw_sb = qkvw[0:HK, :].rearrange("p (c n) -> p c n", c=HC)
        gatew_sb = sb("gatew_sb", [HK, HC, E])
        b2_sb = sb("b2_sb", [E, H])
        tokb_sb = sb("tokb_sb", [TT, H])
        vb_sb = sb("vb_sb", [TT, H])
        qkb_sb = sb("qkb_sb", [HK, 4])
        nscale_sb = sb("nscale_sb", [TT, H])
        gateb_sb = sb("gateb_sb", [TT, E])
        ident = sb("ident", [128, 128])
        clip_mask = sb("clip_mask", [TT, TT])
        before = sb("before", [TT, SLOTS], F16)
        ones = sb("ones", [TT, SLOTS], F16)
        iota_e = sb("iota_e", [TT, E])
        iota_s = sb("iota_s", [TT, SLOTS], F16)
        iota_m = sb("iota_m", [128, MT])
        token_id = sb("token_id", [TT, TILES])
        pad_row = sb("pad_row", [SLOTS, 2])
        lower = sb("lower", [128, E, E])
        eps_sb = sb("eps_sb", [TT, 1])
        minus_half = sb("minus_half", [TT, 2])
        uc = sb("uc", [TT, 2, H])
        x_sb = sb("x_sb", [FK, RING * FC * TT])
        h = sb("h", [TT, TILES, H])
        hn_all = sb("hn_all", [128, TILES * H])
        hn = hn_all[0:TT, :].rearrange("p (i n) -> p i n", i=TILES)
        ln2_all = sb("ln2_all", [128, TILES * H])
        ln2 = ln2_all[0:TT, :].rearrange("p (i n) -> p i n", i=TILES)
        bn = sb("bn", [TT, TILES, 6])
        mv = sb("mv", [TT, TILES, 2])
        mv2 = sb("mv2", [TT, TILES, 2])
        var_eps = sb("var_eps", [TT, TILES])
        rstd = sb("rstd", [TT, TILES])
        var2 = sb("var2", [TT, TILES, 2])
        rstd2 = sb("rstd2", [TT, TILES, 2])
        hT = sb("hT", [HK, 2, HC, TT])
        tT = sb("tT", [HK, 2, HC, TT])
        qk_all = sb("qk_all", [128, 2 * 4 * TT])
        qk = qk_all[0:HK, :].rearrange("p (b m t) -> p b m t", b=2, m=4)
        int_sb = qk_all[:, 0:3 * 160].bitcast(I32).rearrange("p (a n) -> p a n", a=3)
        v = sb("v", [TT, 2, H])
        sm = sb("sm", [TT, TT])
        nmax = sb("nmax", [TT, TILES])
        prob = sb("prob", [TT, TT])
        psums = sb("psums", [TT, TILES])
        rsum = sb("rsum", [TT, TILES])
        probT = sb("probT", [TT, TT])
        logits = sb("logits", [TT, TILES, E])
        top = sb("top", [TT, TILES, 8])
        topi = sb("topi", [TT, TILES, 8], U32)
        topif = sb("topif", [TT, TILES, K])
        nh = TILES * K * E
        hot = tokw[0:TT, 0:nh].rearrange("p (i k e) -> p i k e", i=TILES, k=K)
        prod = tokw[0:TT, nh:2 * nh].rearrange("p (i k e) -> p i k e", i=TILES, k=K)
        mask = sb("mask", [TT, TILES, E], F16)
        dv = sb("dv", [TT, TILES, K])
        ev = sb("ev", [TT, TILES, K])
        es = sb("es", [TT, TILES])
        route = sb("route", [TT, TILES, K])
        comb = sb("comb", [TT, TILES, E])
        comb_prod = qkvw[0:TT, E * E:E * E + K * TILES * E].rearrange("p (k i e) -> p k i e", k=K, i=TILES)
        combT = sb("combT", [E, TILES, TT])
        cnt_c = sb("cnt_c", [E, 4])
        cnt_ci = sb("cnt_ci", [E, 2], I32)
        upto = sb("upto", [E, E])
        iota_c = sb("iota_c", [E, MT])
        ended = sb("ended", [E, MT], F16)
        cnt_i = sb("cnt_i", [128, E], I32)
        cnt_t = sb("cnt_t", [128, E], I32)
        base_prod = qkvw[:, 0:E * E].rearrange("p (e f) -> p e f", e=E)
        base = sb("base", [128, E])
        base_s = sb("base_s", [128, E])
        o = E * E + K * TILES * E
        pos_e = qkvw[0:TT, o:o + TILES * E].rearrange("p (i e) -> p i e", i=TILES)
        o += TILES * E
        pos = qkvw[0:TT, o:o + PAIRS]
        pos_i = qkvw[0:TT, o + PAIRS:o + 4 * PAIRS].bitcast(I32).rearrange("p (a c) -> p a c", a=3)
        pos_f = qkvw[0:TT, o + 4 * PAIRS:o + 6 * PAIRS].rearrange("p (a c) -> p a c", a=2)
        owner = sb("owner", [1, MT], I32)
        pad_now = sb("pad_now", [SLOTS, MT])
        get_row = sb("get_row", [SLOTS, MT], U32)
        put_row = sb("put_row", [SLOTS, MT], U32)
        xg = [hn_all[:, c * ROW:(c + 1) * ROW] for c in range(RING)]
        ysb = [hn_all[:, RING * ROW + c * H:RING * ROW + (c + 1) * H] for c in range(RING)]
        weight = sb("weight", [SLOTS, RING])
        xT = sb("xT", [HK + 1, HC, SLOTS])
        glu, lin, sig, gs = (ln2_all[:, n * I:(n + 1) * I] for n in range(4))
        act_a = tokw[:, 2 * nh:2 * nh + I]
        aT = tokw[:, 2 * nh + I:2 * nh + 2 * I].rearrange("p (c t) -> p c t", c=IC)

        x_ring = x_sb[:, :].rearrange("p (r c t) -> p r c t", r=RING, c=FC)
        half = x_sb[:, :].bitcast(F16)
        nl = PAIRS * SLOTS
        nr = PAIRS * MT
        lo_hot = half[:, 0:nl].rearrange("p (c s) -> p c s", c=PAIRS)
        hi_val = half[:, nl:nl + 2 * nr].rearrange("p (c v m) -> p c v m", c=PAIRS, v=2)

        bank = [ctx.enter_context(nc.psum_tensor(f"bank{n}", [128, 512], F32)) for n in range(8)]
        ps_emb = bank[0][0:TT, 0:H]
        ps_hT = bank[2][0:HK, 0:HC * TT].rearrange("p (c t) -> p c t", c=HC)
        ps_qk = bank[3][0:HK, 0:4 * TT].rearrange("p (c t) -> p c t", c=4)
        ps_v = bank[4][0:TT, 0:H]
        ps_s = bank[5][0:TT, 0:TT]
        ps_pT = bank[6][0:TT, 0:TT]
        ps_o = bank[7][0:TT, 0:H]
        ps_tT = bank[1][0:HK, 0:HC * TT].rearrange("p (c t) -> p c t", c=HC)
        ps_gate = bank[1][0:TT, HC * TT:HC * TT + E]
        ps_cntc = bank[7][0:E, 0:1]
        ps_end = bank[7][0:E, 1:2]
        ps_owner = bank[7][0:1, 2:2 + MT]
        ps_rank = bank[4][0:TT, 0:TILES * E]
        ps_cnt = bank[5][0:128, 0:E]
        ps_rows = bank[6][0:SLOTS, 0:2 * MT]
        ps_cT = [bank[n][0:E, 0:4 * TT].rearrange("p (c t) -> p c t", c=4) for n in (0, 1)]
        ps_b2 = [bank[n][0:TT, 0:2 * H].rearrange("p (c t) -> p c t", c=2) for n in (4, 5, 2, 7)]
        ps_glu = bank[0][:, 0:I]
        ps_lin = bank[1][:, 0:I]
        ps_aT = bank[2][:, 0:IC * SLOTS].rearrange("p (c t) -> p c t", c=IC)
        ps_xT = bank[3][0:HK, 0:HC * SLOTS].rearrange("p (c t) -> p c t", c=HC)
        ps_y = bank[4][:, 0:H]

        s_x = [sem(f"s_x{c}") for c in range(RING)]
        s_first = [sem(f"s_first{n}") for n in range(FIRST)]
        s_small = sem("s_small")
        s_qkvw = sem("s_qkvw")
        s_w1 = sem("s_w1")
        s_w2 = sem("s_w2")
        N_SMALL = 7
        s_pool = sem("s_pool")
        s_const = sem("s_const")
        s_iotas = sem("s_iotas")
        s_emb = sem("s_emb")
        s_h = sem("s_h")
        s_stat = sem("s_stat")
        s_rstd = sem("s_rstd")
        s_hn = sem("s_hn")
        s_hT = sem("s_hT")
        s_hTc = sem("s_hTc")
        s_qk = sem("s_qk")
        s_v = sem("s_v")
        s_qkc = sem("s_qkc")
        s_vc = sem("s_vc")
        s_s = sem("s_s")
        s_sm = sem("s_sm")
        s_nmax = sem("s_nmax")
        s_prob = sem("s_prob")
        s_pT = sem("s_pT")
        s_pTc = sem("s_pTc")
        s_o = sem("s_o")
        s_h2 = sem("s_h2")
        s_stat2 = sem("s_stat2")
        s_rstd2 = sem("s_rstd2")
        s_vb = sem("s_vb")
        s_u = sem("s_u")
        s_t = sem("s_t")
        s_trow = sem("s_trow")
        s_tT = sem("s_tT")
        s_tTc = sem("s_tTc")
        s_gate = sem("s_gate")
        s_logit = sem("s_logit")
        s_top = sem("s_top")
        s_topi = sem("s_topi")
        s_rsum = sem("s_rsum")
        s_bn = sem("s_bn")
        s_dve = sem("s_dve")
        s_mask = sem("s_mask")
        s_rank = sem("s_rank")
        s_dv = sem("s_dv")
        s_ev = sem("s_ev")
        s_route = sem("s_route")
        s_comb = sem("s_comb")
        s_cT = sem("s_cT")
        s_cTc = sem("s_cTc")
        s_b2 = sem("s_b2")
        s_b2c = sem("s_b2c")
        s_cntc = sem("s_cntc")
        s_end = sem("s_end")
        s_ended = sem("s_ended")
        s_own = sem("s_own")
        s_owner = sem("s_owner")
        s_pos = sem("s_pos")
        s_hi = sem("s_hi")
        s_hi_val = sem("s_hi_val")
        s_hot = sem("s_hot")
        s_hot_pool = sem("s_hot_pool")
        s_rows = sem("s_rows")
        s_table = sem("s_table")
        s_base = sem("s_base")
        s_got = [sem(f"s_got{c}") for c in range(RING)]
        s_put = sem("s_put")
        s_base_out = sem("s_base_out")
        s_weight = sem("s_weight")
        s_xT = sem("s_xT")
        s_xTc = sem("s_xTc")
        s_glu = sem("s_glu")
        s_gluc = sem("s_gluc")
        s_sig = sem("s_sig")
        s_lin = sem("s_lin")
        s_linc = sem("s_linc")
        s_gs = sem("s_gs")
        s_a = sem("s_a")
        s_aT = sem("s_aT")
        s_aTc = sem("s_aTc")
        s_y = sem("s_y")
        s_yc = sem("s_yc")
        def wait(eng, s, value):
            if not isinstance(value, int) or value > 0:
                eng.wait_ge(s, value)

        def slot_steps(eng, step):
            whole = (MT - 2) // RING
            for c in range(RING + 1):
                step(0, c)
            with eng.Fori(1, whole) as g:
                for c in range(1, RING + 1):
                    step(g, c)
            for c in range(1, MT - RING * whole):
                step(whole, c)

        block = ctx.enter_context(nc.Block())

        @block.sync
        def _(sp):
            for n in range(FIRST):
                c = slice(n * FC // FIRST, (n + 1) * FC // FIRST)
                sp.dma_start(tokw_sb[:, c, :], tok_w[:, c, :]).then_inc(s_first[n], 16)
                sp.dma_start(x_ring[:, 0, c], x[0][:, c, :]).then_inc(s_first[n], 16)
            def load_expert(e):
                sp.dma_start(w1_sb[0:HK, e * W1E:(e + 1) * W1E], w1[e]).then_inc(s_w1, 16)
                sp.dma_start(w2_sb[:, e * W2E:(e + 1) * W2E], w2[e]).then_inc(s_w2, 16)

            for i in range(1, TILES):
                if i >= RING:
                    sp.wait_ge(s_emb, i - RING + 1)
                sp.dma_start(x_ring[:, i % RING], x[i]).then_inc(s_x[i % RING], 16)
                if i == 1:
                    sp.dma_start(tokb_sb[:, :], tok_b.broadcast_to([TT, H])).then_inc(s_small, 16)
                    sp.dma_start(vb_sb[:, :], v_b.broadcast_to([TT, H])).then_inc(s_small, 16)
                    sp.dma_start(nscale_sb[:, :], norm_scale.broadcast_to([TT, H])).then_inc(s_small, 16)
                    sp.dma_start(gateb_sb[:, :], gate_b.broadcast_to([TT, E])).then_inc(s_small, 16)
                    sp.dma_start(qkb_sb[:, :], qk_b).then_inc(s_small, 16)
                    sp.dma_start(gatew_sb[:, :, :], gate_w).then_inc(s_small, 16)
                    sp.dma_start(b2_sb[:, :], b2).then_inc(s_small, 16)
                    sp.dma_start(qkvw_sb[:, :, :], qkv_w).then_inc(s_qkvw, 16)
                if i == RING - 1:
                    sp.dma_start(w1_sb[HK:HK + 1, :].rearrange("p (e c n) -> p e c n", e=E, c=HC)[:, :, HC - 1, :],
                                 b1).then_inc(s_w1, 16)
                if i >= RING:
                    for e in range(2 * (i - RING), 2 * (i - RING) + 2):
                        load_expert(e)
            for e in range(2 * (TILES - RING), E):
                load_expert(e)
            for i in range(TILES):
                sp.wait_ge(s_t, i + 1)
                sp.dma_start(t_rows[i * TT:(i + 1) * TT, 0:H], hn[:, i, :]).then_inc(s_trow, 16)
            sp.wait_ge(s_w2, 16 * E)
            sp.dma_start(out[TOKENS:TOKENS + SLOTS, :], w2_sb[:, 0:H]).then_inc(s_base_out, 16)
            sp.wait_ge(s_comb, 1)
            sp.dma_start(t_rows.rearrange("(i p) n -> p i n", p=TT)[:, :, H:ROW], comb[:, :, :]).then_inc(s_trow, 16)
            sp.wait_ge(s_b2c, 4)
            sp.dma_start(out[0:TOKENS, :].rearrange("(i p) n -> p i n", p=TT), h[:, :, :]).then_inc(s_base_out, 16)
            sp.wait_ge(s_base_out, 32)
            sp.wait_ge(s_put, 16 * MT)

        @block.gpsimd
        def _(pool):
            n = 0

            def link(ins):
                nonlocal n
                n += 1
                ins.then_inc(s_pool, 1)
                pool.wait_ge(s_pool, n)

            g = nc.gpsimd
            link(g.memset(eps_sb[:, :], EPS))
            link(g.memset(minus_half[:, :], -0.5))
            link(g.memset(ident[:, :], 0.0))
            g.affine_select(out=ident[:, :], in_=ident[:, :], compare_op=ALU.not_equal, fill=1.0, base=0,
                            pattern=[[-1, 128]], channel_multiplier=1).then_inc(s_const, 1)
            link(g.memset(clip_mask[:, :], 0.0))
            cm = clip_mask[:, :].rearrange("p (b w) -> p b w", w=SEQ)
            link(g.affine_select(out=cm, in_=cm, compare_op=ALU.is_ge, fill=OFF_CLIP, base=0,
                                 pattern=[[-SEQ, TT // SEQ], [0, SEQ]], channel_multiplier=1))
            g.affine_select(out=cm, in_=cm, compare_op=ALU.is_ge, fill=OFF_CLIP, base=SEQ - 1,
                            pattern=[[SEQ, TT // SEQ], [0, SEQ]], channel_multiplier=-1).then_inc(s_const, 1)
            g.memset(ones[:, :], 1.0).then_inc(s_const, 1)
            link(g.memset(before[:, :], 1.0))
            g.affine_select(out=before[:, :], in_=before[:, :], compare_op=ALU.is_ge, fill=0.0, base=-1,
                            pattern=[[1, SLOTS]], channel_multiplier=-1).then_inc(s_const, 1)
            link(g.memset(lower[:, :, :], 1.0))
            g.affine_select(out=lower[:, :, :], in_=lower[:, :, :], compare_op=ALU.is_ge, fill=0.0, base=-1,
                            pattern=[[1, E], [-1, E]], channel_multiplier=0).then_inc(s_const, 1)
            link(g.memset(upto[:, :], 1.0))
            g.affine_select(out=upto[:, :], in_=upto[:, :], compare_op=ALU.is_ge, fill=0.0, base=0,
                            pattern=[[1, E]], channel_multiplier=-1).then_inc(s_const, 1)
            pool.wait_ge(s_const, 6)
            g.memset(xT[HK:HK + 1, :, :], 1.0).then_inc(s_const, 1)
            pool.wait_ge(s_const, 7)
            g.iota(int_sb[:, 0, :], pattern=[[1, 160]], base=0, channel_multiplier=0).then_inc(s_iotas, 1)
            g.iota(int_sb[:, 1, 0:TILES], pattern=[[TT, TILES]], base=0, channel_multiplier=1).then_inc(s_iotas, 1)
            g.iota(int_sb[:, 2, 0:1], pattern=[[1, 1]], base=TOKENS, channel_multiplier=1).then_inc(s_iotas, 1)

            def root(i):
                pool.wait_ge(s_stat, i + 1)
                link(g.tensor_tensor(var_eps[:, i:i + 1], mv[:, i, 1:2], eps_sb[:, :], ALU.add))
                g.tensor_tensor(rstd[:, i:i + 1], var_eps[:, i:i + 1], minus_half[:, 0:1], ALU.pow).then_inc(s_rstd, 1)

            def v_bias(i):
                pool.wait_ge(s_hn, i + 1)
                g.tensor_tensor(h[:, i, :], h[:, i, :], vb_sb[:, :], ALU.add).then_inc(s_vb, 1)

            def root2(i):
                pool.wait_ge(s_stat2, i + 1)
                g.tensor_scalar(var2[:, i, 0:1], mv2[:, i, 1:2], 1.0, EPS, ALU.mult, ALU.add)
                link(g.tensor_scalar(var2[:, i, 1:2], mv2[:, i, 1:2], 1.0 + EPS, EPS * EPS, ALU.mult, ALU.add))
                g.tensor_tensor(rstd2[:, i, :], var2[:, i, :], minus_half[:, :], ALU.pow).then_inc(s_rstd2, 1)

            def add_norm2(i):
                pool.wait_ge(s_rstd2, i + 1)
                link(g.tensor_scalar(ln2[:, i, :], h[:, i, :], mv2[:, i, 0:1], rstd2[:, i, 0:1],
                                     ALU.subtract, ALU.mult))
                pool.wait_ge(s_u, i + 1)
                g.tensor_tensor(h[:, i, :], h[:, i, :], ln2[:, i, :], ALU.add).then_inc(s_base, 1)

            pool.wait_ge(s_small, 16 * N_SMALL)
            for i in range(AHEAD):
                root(i)
                v_bias(i)
            for i in range(TILES + 2):
                if i >= 2:
                    root2(i - 2)
                if i + AHEAD < TILES:
                    root(i + AHEAD)
                if i >= 2:
                    add_norm2(i - 2)
                if i + AHEAD < TILES:
                    v_bias(i + AHEAD)
            pool.wait_ge(s_route, 1)
            for k in range(K):
                ins = g.tensor_tensor(comb_prod[:, k], hot[:, :, k, :],
                                      route[:, :, k].unsqueeze(2).to_broadcast([TT, TILES, E]), ALU.mult)
            link(ins)
            link(g.tensor_tensor(comb_prod[:, 0:2], comb_prod[:, 0:2], comb_prod[:, 2:4], ALU.add))
            g.tensor_tensor(comb[:, :, :], comb_prod[:, 0], comb_prod[:, 1], ALU.add).then_inc(s_comb, 1)
            pool.wait_ge(s_pos, 1)
            for c in range(PAIRS - POOL_HOTS, PAIRS):
                g.tensor_scalar(lo_hot[:, c, :], iota_s[:, :], pos_f[:, 0, c:c + 1], None,
                                ALU.is_equal).then_inc(s_hot_pool, 1)

            def gather(m, slot):
                g.indirect_dma_start(out=xg[slot], out_offset=None, in_=t_rows,
                                     in_offset=bass.IndirectOffsetOnAxis(ap=get_row[:, m:m + 1], axis=0),
                                     ).then_inc(s_got[slot], 16)

            def scatter(m, slot):
                if m > 0:
                    pool.wait_ge(s_put, 16 * m)
                g.indirect_dma_start(out=out,
                                     out_offset=bass.IndirectOffsetOnAxis(ap=put_row[:, m:m + 1], axis=0),
                                     in_=ysb[slot], in_offset=None, compute_op=ALU.add,
                                     ).then_inc(s_put, 16)

            pool.wait_ge(s_table, 1)
            pool.wait_ge(s_trow, 16 * (TILES + 1))
            for m in range(2):
                gather(m, m)

            for j in range(MT):
                if j + 2 < MT:
                    if j > 0:
                        pool.wait_ge(s_xT, j)
                        pool.wait_ge(s_weight, j)
                    gather(j + 2, (j + 2) % RING)
                if j > 0:
                    if j == 1:
                        pool.wait_ge(s_table, 2)
                        pool.wait_ge(s_base_out, 32)
                    pool.wait_ge(s_yc, j)
                    scatter(j - 1, (j - 1) % RING)
            pool.wait_ge(s_yc, MT)
            scatter(MT - 1, (MT - 1) % RING)

        @block.scalar
        def _(act):
            a = nc.scalar
            def copy_hT(i):
                act.wait_ge(s_hT, i + 1)
                if i >= 2:
                    act.wait_ge(s_v, i - 1)
                a.copy(hT[:, i % 2], ps_hT).then_inc(s_hTc, 1)

            def softmax(i):
                act.wait_ge(s_nmax, i + 1)
                if i >= 1:
                    act.wait_ge(s_pT, i)
                a.activation(prob[:, :], sm[:, :], ACT.Exp, bias=nmax[:, i:i + 1],
                             accum_out=psums[:, i:i + 1]).then_inc(s_prob, 1)

            def copy_pT(i):
                act.wait_ge(s_pT, i + 1)
                if i >= 1:
                    act.wait_ge(s_o, i)
                a.copy(probT[:, :], ps_pT).then_inc(s_pTc, 1)

            def copy_v(i):
                act.wait_ge(s_v, i + 1)
                if i >= 2:
                    act.wait_ge(s_o, i - 1)
                a.copy(v[:, i % 2, :], ps_v).then_inc(s_vc, 1)

            def copy_tT(i):
                act.wait_ge(s_tT, i + 1)
                if i >= 2:
                    act.wait_ge(s_gate, i - 1)
                a.copy(tT[:, i % 2], ps_tT).then_inc(s_tTc, 1)

            copy_hT(0)
            for i in range(TILES + 3):
                if 1 <= i <= TILES:
                    softmax(i - 1)
                    copy_pT(i - 1)
                if i >= 3:
                    copy_tT(i - 3)
                if i < TILES:
                    copy_v(i)
                if i + 1 < TILES:
                    copy_hT(i + 1)
            act.wait_ge(s_dv, 1)
            a.activation(ev[:, :, :], dv[:, :, :], ACT.Exp).then_inc(s_ev, 1)
            for n in range(2):
                act.wait_ge(s_cT, n + 1)
                a.copy(combT[:, 4 * n:4 * n + 4, :], ps_cT[n]).then_inc(s_cTc, 1)

            act.wait_ge(s_hi, 1)
            for i in range(TILES):
                c = slice(K * i, K * i + K)
                a.activation(hi_val[:, c, 0, :], hi_val[:, c, 1, :], ACT.Copy,
                             scale=token_id[:, i:i + 1]).then_inc(s_hi_val, 1)
            act.wait_ge(s_owner, 1)

            def copy_xT(j, slot):
                act.wait_ge(s_xT, j + 1)
                wait(act, s_lin, j)
                a.copy(xT[0:HK, :, :], ps_xT).then_inc(s_xTc, 1)
                e = act.value_load(owner[0:1, bass.ds(j, 1) if not isinstance(j, int) else slice(j, j + 1)],
                                   min_val=0, max_val=E - 1)
                wait(act, s_yc, j + 1 - RING)
                a.copy(weight[:, slot:slot + 1], xg[slot][:, bass.ds(e + H, 1)]).then_inc(s_weight, 1)

            def copy_aT(j):
                act.wait_ge(s_aT, j + 1)
                wait(act, s_y, j)
                a.copy(aT[:, :, :], ps_aT).then_inc(s_aTc, 1)

            def copy_y(j, slot):
                act.wait_ge(s_y, j + 1)
                wait(act, s_put, 16 * (j + 1 - RING))
                act.wait_ge(s_weight, j + 1)
                a.activation(ysb[slot], ps_y, ACT.Copy, scale=weight[:, slot:slot + 1]).then_inc(s_yc, 1)

            copy_xT(0, 0)

            def step(gi, c):
                j = RING * gi + c
                first = isinstance(j, int) and j == 0
                if not first:
                    copy_aT(j - 1)
                act.wait_ge(s_gluc, j + 1)
                wait(act, s_gs, j)
                a.activation(sig, glu, ACT.Sigmoid, scale=ALPHA).then_inc(s_sig, 1)
                if not (isinstance(j, int) and j == MT - 1):
                    copy_xT(j + 1, (c + 1) % RING)
                if not first:
                    copy_y(j - 1, (c - 1) % RING)

            slot_steps(act, step)
            copy_aT(MT - 1)
            copy_y(MT - 1, (MT - 1) % RING)

        @block.vector
        def _(dve):
            d = nc.vector
            n = 0

            def link(ins):
                nonlocal n
                n += 1
                ins.then_inc(s_dve, 1)
                dve.wait_ge(s_dve, n)

            dve.wait_ge(s_iotas, 3)
            d.tensor_copy(iota_e[:, :], int_sb[0:TT, 0, 0:E])
            d.tensor_copy(iota_s[:, :], int_sb[0:TT, 0, 0:SLOTS])
            d.tensor_copy(iota_m[:, :], int_sb[:, 0, 0:MT])
            d.tensor_copy(token_id[:, :], int_sb[0:TT, 1, 0:TILES])
            d.tensor_copy(iota_c[:, :], int_sb[0:E, 0, 0:MT])
            link(d.tensor_copy(pad_row[:, 0:1], int_sb[:, 2, 0:1]))
            d.tensor_scalar(pad_row[:, 1:2], pad_row[:, 0:1], -1.0, None, ALU.mult)

            dve.wait_ge(s_small, 16 * N_SMALL)

            def embed(i):
                dve.wait_ge(s_emb, i + 1)
                d.tensor_tensor(h[:, i, :], ps_emb, tokb_sb[:, :], ALU.add).then_inc(s_h, 1)
                dve.wait_ge(s_h, i + 1)
                link(d.bn_stats(bn[:, i, :], h[:, i, :]))
                d.bn_aggr(mv[:, i, :], bn[:, i, :]).then_inc(s_stat, 1)

            def normalise(i):
                dve.wait_ge(s_rstd, i + 1)
                d.tensor_scalar(hn[:, i, :], h[:, i, :], mv[:, i, 0:1], rstd[:, i:i + 1],
                                ALU.subtract, ALU.mult).then_inc(s_hn, 1)

            def scores(i):
                dve.wait_ge(s_s, i + 1)
                if i >= 1:
                    dve.wait_ge(s_prob, i)
                d.scalar_tensor_tensor(out=sm[:, :], in0=ps_s, scalar=SCALE, in1=clip_mask[:, :],
                                       op0=ALU.mult, op1=ALU.add).then_inc(s_sm, 1)
                if i >= 1:
                    d.reciprocal(rsum[:, i - 1:i], psums[:, i - 1:i]).then_inc(s_rsum, 1)
                dve.wait_ge(s_sm, i + 1)
                d.tensor_reduce(nmax[:, i:i + 1], sm[:, :], AX.X, ALU.max, negate=True).then_inc(s_nmax, 1)

            def copy_qk(i):
                dve.wait_ge(s_qk, i + 1)
                if i >= 2:
                    dve.wait_ge(s_s, i - 1)
                d.tensor_tensor(qk[:, i % 2], ps_qk, qkb_sb[:, :].unsqueeze(2).to_broadcast([HK, 4, TT]),
                                ALU.add).then_inc(s_qkc, 1)

            def residual_and_pick(i, j):
                if i == TILES - 1:
                    dve.wait_ge(s_prob, i + 1)
                    d.reciprocal(rsum[:, i:i + 1], psums[:, i:i + 1]).then_inc(s_rsum, 1)
                if i < TILES:
                    dve.wait_ge(s_rsum, i + 1)
                    dve.wait_ge(s_vb, i + 1)
                    dve.wait_ge(s_o, i + 1)
                    d.scalar_tensor_tensor(out=h[:, i, :], in0=ps_o, scalar=rsum[:, i:i + 1], in1=h[:, i, :],
                                           op0=ALU.mult, op1=ALU.add).then_inc(s_h2, 1)
                if j >= 0:
                    dve.wait_ge(s_gate, j + 1)
                    d.tensor_tensor(logits[:, j, :], ps_gate, gateb_sb[:, :], ALU.add).then_inc(s_logit, 1)
                if i < TILES:
                    dve.wait_ge(s_h2, i + 1)
                    d.bn_stats(bn[:, i, :], h[:, i, :]).then_inc(s_bn, 1)
                if j >= 0:
                    dve.wait_ge(s_logit, j + 1)
                    d.max(top[:, j, :], logits[:, j, :]).then_inc(s_top, 1)
                if i < TILES:
                    dve.wait_ge(s_bn, i + 1)
                    d.bn_aggr(mv2[:, i, :], bn[:, i, :]).then_inc(s_stat2, 1)
                if j >= 0:
                    dve.wait_ge(s_top, j + 1)
                    d.max_index(topi[:, j, :], top[:, j, :], logits[:, j, :]).then_inc(s_topi, 1)
                if i < TILES:
                    dve.wait_ge(s_stat2, i + 1)
                    if i >= 2:
                        dve.wait_ge(s_t, i - 1)
                    d.scalar_tensor_tensor(out=uc[:, i % 2, :], in0=h[:, i, :], scalar=mv2[:, i, 0:1],
                                           in1=nscale_sb[:, :], op0=ALU.subtract, op1=ALU.mult).then_inc(s_u, 1)

            def normalise2(i):
                dve.wait_ge(s_rstd2, i + 1)
                dve.wait_ge(s_u, i + 1)
                d.tensor_scalar(hn[:, i, :], uc[:, i % 2, :], rstd2[:, i, 1:2], None, ALU.mult).then_inc(s_t, 1)

            for i in range(AHEAD):
                embed(i)
                normalise(i)
            dve.wait_ge(s_const, 2)
            for i in range(TILES + 4):
                if 1 <= i <= TILES:
                    scores(i - 1)
                if i >= 2:
                    residual_and_pick(i - 2, i - 4)
                if i + AHEAD < TILES:
                    embed(i + AHEAD)
                if 2 <= i < TILES + 2:
                    normalise2(i - 2)
                if i < TILES:
                    copy_qk(i)
                if i + AHEAD < TILES:
                    normalise(i + AHEAD)
            dve.wait_ge(s_topi, TILES)

            d.tensor_tensor(dv[:, :, :], top[:, :, 0:K], top[:, :, 0:1].to_broadcast([TT, TILES, K]),
                            ALU.subtract).then_inc(s_dv, 1)
            link(d.tensor_copy(topif[:, :, :], topi[:, :, 0:K]))
            hot3 = tokw[0:TT, 0:nh].rearrange("p (c e) -> p c e", e=E)
            prod3 = tokw[0:TT, nh:2 * nh].rearrange("p (c e) -> p c e", e=E)
            link(d.tensor_tensor(hot3, topif[:, :, :].rearrange("p i k -> p (i k)").unsqueeze(2)
                                 .to_broadcast([TT, PAIRS, E]),
                                 iota_e[:, :].unsqueeze(1).to_broadcast([TT, PAIRS, E]), ALU.is_equal))
            with nc.allow_low_precision("counts of 0 and 1 are exact"):
                d.tensor_reduce(mask[:, :, :], hot[:, :, :, :].rearrange("p i k e -> p i e k"), AX.X,
                                ALU.add).then_inc(s_mask, 1)
            dve.wait_ge(s_ev, 1)
            link(d.tensor_reduce(es[:, :], ev[:, :, :], AX.X, ALU.add))
            link(d.reciprocal(es[:, :], es[:, :]))
            d.tensor_tensor(route[:, :, :], ev[:, :, :], es[:, :].unsqueeze(2).to_broadcast([TT, TILES, K]),
                            ALU.mult).then_inc(s_route, 1)
            dve.wait_ge(s_rank, 2)
            d.tensor_scalar(cnt_ci[:, 0:1], ps_cntc, float(SLOTS - 1), None, ALU.add)
            link(d.tensor_scalar(cnt_i[:, :], ps_cnt, float(SLOTS - 1), None, ALU.add))
            d.tensor_scalar(cnt_ci[:, 1:2], cnt_ci[:, 0:1], SLOT_BITS, None, ALU.arith_shift_right)
            link(d.tensor_scalar(cnt_t[:, :], cnt_i[:, :], SLOT_BITS, None, ALU.arith_shift_right))
            d.tensor_copy(cnt_c[:, 0:1], cnt_ci[:, 1:2]).then_inc(s_cntc, 1)
            link(d.tensor_tensor(base_prod[:, :, :], lower[:, :, :],
                                 cnt_t[:, :].unsqueeze(1).to_broadcast([128, E, E]), ALU.mult))
            link(d.tensor_reduce(base[:, :], base_prod[:, :, :], AX.X, ALU.add))
            link(d.tensor_scalar(base_s[:, :], base[:, :], float(SLOTS), None, ALU.mult))
            dve.wait_ge(s_rank, 3)
            link(d.tensor_tensor(pos_e[:, :, :], ps_rank.rearrange("p (i e) -> p i e", e=E),
                                 base_s[0:TT, :].unsqueeze(1).to_broadcast([TT, TILES, E]), ALU.add))
            link(d.tensor_tensor(prod, hot, pos_e[:, :, :].unsqueeze(2).to_broadcast([TT, TILES, K, E]), ALU.mult))
            link(d.tensor_reduce(pos, prod3, AX.X, ALU.add))
            link(d.tensor_copy(pos_i[:, 0, :], pos))
            d.tensor_scalar(pos_i[:, 1, :], pos_i[:, 0, :], SLOTS - 1, None, ALU.bitwise_and)
            link(d.tensor_scalar(pos_i[:, 2, :], pos_i[:, 0, :], SLOT_BITS, None, ALU.arith_shift_right))
            d.tensor_copy(pos_f[:, :, :], pos_i[:, 1:3, :]).then_inc(s_pos, 1)
            dve.wait_ge(s_pos, 1)
            d.tensor_tensor(hi_val[:, :, 1, :], pos_f[:, 1, :].unsqueeze(2).to_broadcast([TT, PAIRS, MT]),
                            iota_m[0:TT, :].unsqueeze(1).to_broadcast([TT, PAIRS, MT]),
                            ALU.is_equal).then_inc(s_hi, 1)
            dve.wait_ge(s_end, 1)
            link(d.tensor_copy(cnt_c[:, 1:2], ps_end))
            d.tensor_scalar(ended[:, :], iota_c[:, :], cnt_c[:, 1:2], None, ALU.is_ge).then_inc(s_ended, 1)
            for c in range(PAIRS - POOL_HOTS):
                d.tensor_scalar(lo_hot[:, c, :], iota_s[:, :], pos_f[:, 0, c:c + 1], None,
                                ALU.is_equal).then_inc(s_hot, 1)
            dve.wait_ge(s_own, 1)
            d.tensor_scalar(owner[:, :], ps_owner, float(E - 1), None, ALU.min).then_inc(s_owner, 1)
            dve.wait_ge(s_rows, 1)
            d.tensor_copy(get_row[:, :], ps_rows[:, 0:MT]).then_inc(s_table, 1)
            link(d.tensor_scalar(pad_now[:, :], ps_rows[:, MT:2 * MT], pad_row[:, 1:2], pad_row[:, 0:1],
                                 ALU.mult, ALU.add))
            d.tensor_tensor(put_row[:, :], pad_now[:, :], ps_rows[:, 0:MT], ALU.add).then_inc(s_table, 1)
            dve.wait_ge(s_base, TILES)
            for q in range(4):
                dve.wait_ge(s_b2, q + 1)
                d.tensor_tensor(h[:, 2 * q:2 * q + 2, :], h[:, 2 * q:2 * q + 2, :], ps_b2[q],
                                ALU.add).then_inc(s_b2c, 1)

            def step(gi, c):
                j = RING * gi + c
                dve.wait_ge(s_glu, j + 1)
                wait(dve, s_gs, j)
                d.tensor_scalar(glu, ps_glu, LIMIT, None, ALU.min).then_inc(s_gluc, 1)
                dve.wait_ge(s_sig, j + 1)
                wait(dve, s_a, j)
                d.tensor_tensor(gs, glu, sig, ALU.mult).then_inc(s_gs, 1)
                dve.wait_ge(s_lin, j + 1)
                d.tensor_scalar(lin, ps_lin, LIMIT, -LIMIT, ALU.min, ALU.max).then_inc(s_linc, 1)
                dve.wait_ge(s_linc, j + 1)
                dve.wait_ge(s_gs, j + 1)
                wait(dve, s_aT, j)
                d.scalar_tensor_tensor(out=act_a, in0=lin, scalar=1.0, in1=gs,
                                       op0=ALU.add, op1=ALU.mult).then_inc(s_a, 1)

            slot_steps(dve, step)

        @block.tensor
        def _(pe):
            t = nc.tensor

            def turn_h(i):
                pe.wait_ge(s_hn, i + 1)
                if i >= 1:
                    pe.wait_ge(s_hTc, i)
                for c in range(HC):
                    ins = t.transpose(ps_hT[:, c, :], hn[:, i, c * HK:(c + 1) * HK], ident[0:TT, 0:TT])
                ins.then_inc(s_hT, 1)

            def embed(i):
                if i >= 1:
                    pe.wait_ge(s_x[i % RING], 16 * (i // RING + (i % RING > 0)))
                    pe.wait_ge(s_h, i)
                for c in range(FC):
                    if i == 0 and c * FIRST % FC == 0:
                        pe.wait_ge(s_first[c * FIRST // FC], 32)
                    ins = t.matmul(ps_emb, x_ring[:, i % RING, c, :], tokw_sb[:, c, :],
                                   start=(c == 0), stop=(c == FC - 1))
                ins.then_inc(s_emb, 1)

            def query_key(i):
                pe.wait_ge(s_hTc, i + 1)
                if i == 0:
                    pe.wait_ge(s_qkvw, 16)
                if i >= 1:
                    pe.wait_ge(s_qkc, i)
                for m in range(4):
                    for c in range(HC):
                        ins = t.matmul(ps_qk[:, m, :], qkvw_sb[:, c, m * HK:(m + 1) * HK], hT[:, i % 2, c, :],
                                       start=(c == 0), stop=(c == HC - 1))
                ins.then_inc(s_qk, 1)

            def value(i):
                if i >= 1:
                    pe.wait_ge(s_vc, i)
                for c in range(HC):
                    ins = t.matmul(ps_v, hT[:, i % 2, c, :], qkvw_sb[:, c, 2 * H:3 * H],
                                   start=(c == 0), stop=(c == HC - 1))
                ins.then_inc(s_v, 1)

            def score(i):
                pe.wait_ge(s_qkc, i + 1)
                if i >= 1:
                    pe.wait_ge(s_sm, i)
                for c in range(HC):
                    ins = t.matmul(ps_s, qk[:, i % 2, c, :], qk[:, i % 2, HC + c, :],
                                   start=(c == 0), stop=(c == HC - 1))
                ins.then_inc(s_s, 1)

            def turn_p(i):
                pe.wait_ge(s_prob, i + 1)
                if i >= 1:
                    pe.wait_ge(s_pTc, i)
                t.transpose(ps_pT, prob[:, :], ident[0:TT, 0:TT]).then_inc(s_pT, 1)

            def context(i):
                pe.wait_ge(s_pTc, i + 1)
                pe.wait_ge(s_vc, i + 1)
                if i >= 1:
                    pe.wait_ge(s_h2, i)
                t.matmul(ps_o, probT[:, :], v[:, i % 2, :], start=True, stop=True).then_inc(s_o, 1)

            def turn_t(i):
                pe.wait_ge(s_t, i + 1)
                if i >= 1:
                    pe.wait_ge(s_logit, i)
                for c in range(HC):
                    ins = t.transpose(ps_tT[:, c, :], hn[:, i, c * HK:(c + 1) * HK], ident[0:TT, 0:TT])
                ins.then_inc(s_tT, 1)

            def gate(i):
                pe.wait_ge(s_tTc, i + 1)
                for c in range(HC):
                    ins = t.matmul(ps_gate, tT[:, i % 2, c, :], gatew_sb[:, c, :],
                                   start=(c == 0), stop=(c == HC - 1))
                ins.then_inc(s_gate, 1)

            for i in range(AHEAD):
                embed(i)
            pe.wait_ge(s_const, 7)
            pe.wait_ge(s_small, 16 * N_SMALL)
            turn_h(0)
            for i in range(TILES + 3):
                if 1 <= i <= TILES:
                    score(i - 1)
                if i + AHEAD < TILES:
                    embed(i + AHEAD)
                if i < TILES:
                    query_key(i)
                if 1 <= i <= TILES:
                    turn_p(i - 1)
                if i >= 3:
                    turn_t(i - 3)
                if i < TILES:
                    value(i)
                if 1 <= i <= TILES:
                    context(i - 1)
                if i + 1 < TILES:
                    turn_h(i + 1)
                if i >= 3:
                    gate(i - 3)

            pe.wait_ge(s_mask, 1)
            m2 = mask[:, :, :].rearrange("p i e -> p (i e)")
            for i in range(TILES):
                ins = t.matmul(ps_cnt, ones[:, :], mask[:, i, :], start=(i == 0), stop=(i == TILES - 1))
            ins.then_inc(s_rank, 1)
            for i in range(TILES):
                ins = t.matmul(ps_cntc, mask[:, i, :], ones[:, 0:1], start=(i == 0), stop=(i == TILES - 1))
            ins.then_inc(s_rank, 1)
            ins = t.matmul(ps_rank, before[:, 0:TT], m2, start=True, stop=False)
            for s in range(1, TILES):
                ins = t.matmul(ps_rank[:, s * E:TILES * E], ones[:, 0:TT], m2[:, 0:(TILES - s) * E],
                               start=False, stop=(s == TILES - 1))
            ins.then_inc(s_rank, 1)
            pe.wait_ge(s_cntc, 1)
            t.matmul(ps_end, upto[:, :], cnt_c[:, 0:1], start=True, stop=True).then_inc(s_end, 1)
            pe.wait_ge(s_comb, 1)
            pe.wait_ge(s_logit, TILES)
            for n in range(2):
                for i in range(4):
                    ins = t.transpose(ps_cT[n][:, i, :], comb[:, 4 * n + i, :], ident[0:TT, 0:TT])
                ins.then_inc(s_cT, 1)
            pe.wait_ge(s_ended, 1)
            t.matmul(ps_owner, ones[0:E, 0:1], ended[:, :], start=True, stop=True).then_inc(s_own, 1)
            for c in range(PAIRS):
                if c < PAIRS - POOL_HOTS:
                    pe.wait_ge(s_hot, c + 1)
                else:
                    pe.wait_ge(s_hot_pool, c + 1 - (PAIRS - POOL_HOTS))
                pe.wait_ge(s_hi_val, c // K + 1)
                ins = t.matmul(ps_rows, lo_hot[:, c, :], hi_val[:, c, :, :],
                               start=(c == 0), stop=(c == PAIRS - 1))
            ins.then_inc(s_rows, 1)
            pe.wait_ge(s_owner, 1)
            pe.wait_ge(s_pos, 1)
            for q in range(4):
                pe.wait_ge(s_cTc, q // 2 + 1)
                for i in range(2):
                    ins = t.matmul(ps_b2[q][:, i, :], combT[:, 2 * q + i, :], b2_sb[:, :],
                                   start=True, stop=True)
                ins.then_inc(s_b2, 1)

            pe.wait_ge(s_w1, 16 * (E + 1))
            pe.wait_ge(s_w2, 16 * E)

            def turn_x(slot, uses):
                pe.wait_ge(s_got[slot], 16 * uses)
                for c in range(HC):
                    ins = t.transpose(ps_xT[:, c, :], xg[slot][:, c * HK:(c + 1) * HK], ident[:, :])
                ins.then_inc(s_xT, 1)

            def expert(j):
                return pe.value_load(owner[0:1, bass.ds(j, 1) if not isinstance(j, int) else slice(j, j + 1)],
                                     min_val=0, max_val=E - 1)

            def up(e, part, dst):
                for c in range(HC):
                    rows = HK + (c == HC - 1)
                    ins = t.matmul(dst, xT[0:rows, c, :],
                                   w1_sb[0:rows, bass.ds(e * W1E + (2 * c + part) * I, I)],
                                   start=(c == 0), stop=(c == HC - 1))
                return ins

            def turn_a(j):
                pe.wait_ge(s_a, j + 1)
                wait(pe, s_aTc, j)
                for c in range(IC):
                    ins = t.transpose(ps_aT[:, c, :], act_a[:, c * 128:(c + 1) * 128], ident[:, :])
                ins.then_inc(s_aT, 1)

            def down(e, j):
                pe.wait_ge(s_aTc, j + 1)
                wait(pe, s_yc, j)
                for c in range(IC):
                    ins = t.matmul(ps_y, aT[:, c, :], w2_sb[:, bass.ds(e * W2E + c * H, H)],
                                   start=(c == 0), stop=(c == IC - 1))
                ins.then_inc(s_y, 1)

            def step(gi, c):
                j = RING * gi + c
                first = isinstance(j, int) and j == 0
                last = isinstance(j, int) and j == MT - 1
                e = expert(j)
                pe.wait_ge(s_xTc, j + 1)
                wait(pe, s_gluc, j)
                up(e, 0, ps_glu).then_inc(s_glu, 1)
                if not first:
                    if isinstance(j, int) and j == 1:
                        pe.wait_ge(s_b2c, 4)
                    turn_a(j - 1)
                wait(pe, s_linc, j)
                up(e, 1, ps_lin).then_inc(s_lin, 1)
                if not last:
                    turn_x((c + 1) % RING, gi + (c + 1) // RING + 1)
                if not first:
                    down(expert(j - 1), j - 1)

            turn_x(0, 1)
            slot_steps(pe, step)
            turn_a(MT - 1)
            down(expert(MT - 1), MT - 1)


def kernel(**inputs):
    import numpy as np
    import concourse.bacc as bacc
    from concourse.bass_utils import run_bass_kernel_spmd

    a = {k: np.asarray(v) for k, v in inputs.items()}
    x = a["x"][:, :, :SEQ * PATCH].reshape(TILES, CLIPS // TILES, CHANNELS, SEQ, PATCH)
    x = x.transpose(0, 2, 4, 1, 3).reshape(TILES, FC, FK, TT).transpose(0, 2, 1, 3)
    w1 = a["L0_ffn_mlp1_w"].reshape(E, I, 2, HC, HK).transpose(0, 4, 3, 2, 1).reshape(E, HK, W1E)
    b1 = a["L0_ffn_mlp1_b"].reshape(E, I, 2).transpose(0, 2, 1).reshape(1, E, 2 * I)
    w2 = a["L0_ffn_mlp2_w"].reshape(E, H, IC, 128).transpose(0, 3, 2, 1).reshape(E, 128, W2E)
    arrays = {
        "x": x,
        "tok_w": a["L0_tok_W"].reshape(H, FC, FK).transpose(2, 1, 0),
        "tok_b": a["L0_tok_b"].reshape(1, H),
        "qkv_w": a["L0_attn_W_qkv"].reshape(HC, HK, 3 * H).transpose(1, 0, 2),
        "qk_b": a["L0_attn_b_qkv"][:2 * H].reshape(4, HK).transpose(1, 0),
        "v_b": a["L0_attn_b_qkv"][2 * H:].reshape(1, H),
        "norm_scale": a["L0_ffn_norm_scale"].reshape(1, H),
        "gate_w": a["L0_ffn_gate_w"].reshape(E, HC, HK).transpose(2, 1, 0),
        "gate_b": a["L0_ffn_gate_b"].reshape(1, E),
        "w1": w1,
        "b1": b1,
        "w2": w2,
        "b2": a["L0_ffn_mlp2_b"],
    }
    arrays = {f"in_{k}": np.ascontiguousarray(v) for k, v in arrays.items()}
    nc = bacc.Bacc("TRN2", target_bir_lowering=False, num_devices=1)
    args = [nc.dram_tensor(k, v.shape, mybir.dt.from_np(v.dtype), kind="ExternalInput").ap()
            for k, v in arrays.items()]
    out = nc.dram_tensor("out", (TOKENS + SLOTS, H), F32, kind="ExternalOutput").ap()
    audio_tower_kernel(nc, *args, out)
    r = run_bass_kernel_spmd(nc, [arrays], core_ids=[0])
    return r.results[0]["out"][:TOKENS].reshape(CLIPS, SEQ, H)
```

```python
from contextlib import ExitStack

import concourse.bass as bass
from concourse import mybir

F32 = mybir.dt.float32
F16 = mybir.dt.float16
I32 = mybir.dt.int32
U32 = mybir.dt.uint32
ALU = mybir.AluOpType
ACT = mybir.ActivationFunctionType
AX = mybir.AxisListType

CLIPS, CHANNELS, PATCH, SEQ = 64, 90, 16, 15
TOKENS = CLIPS * SEQ
TILES = 8
TT = TOKENS // TILES
FEAT = CHANNELS * PATCH
FC = 12
FK = FEAT // FC
H = 192
HC = 2
HK = H // HC
E, K, I = 16, 4, 384
IC = I // 128
SLOTS = 128
SLOT_BITS = 7
MT = TOKENS * K // SLOTS + E - 1
PAIRS = TILES * K
AHEAD = 2
EPS = 1e-5
LIMIT, ALPHA = 7.0, 1.702
SCALE = 1.0 / float(H) ** 0.5
OFF_CLIP = -1.0e30
ROW = H + E
W1E = HC * 2 * I
W2E = IC * H
RING = 3
UNROLL = 2 * RING
FIRST = (0, 2, 6, FC)
EARLY = TILES - 2
POOL_EVERY = 3


def audio_tower_kernel(nc, x, tok_w, tok_b, qkv_w, qk_b, v_b, norm_scale, gate_w, gate_b,
                       w1, b1, w2, b2, out):
    ctx = ExitStack()
    with ctx:
        def sb(name, shape, dt=F32):
            return ctx.enter_context(nc.sbuf_tensor(name, shape, dt))

        def sem(name):
            return ctx.enter_context(nc.semaphore(name))

        t_rows = nc.dram_tensor("t_rows", (TOKENS, ROW), F32).ap()

        w1_sb = sb("w1_sb", [128, E * W1E])
        w2_sb = sb("w2_sb", [128, E * W2E])
        tokw = sb("tokw", [128, FC * H])
        tokw_sb = tokw[0:FK, :].rearrange("p (c n) -> p c n", c=FC)
        qkvw = sb("qkvw", [128, HC * (3 * H + 2)])
        qkvw_sb = qkvw[0:HK, :].rearrange("p (c n) -> p c n", c=HC)
        gatew_sb = sb("gatew_sb", [HK, HC, E])
        b2_sb = sb("b2_sb", [E, H])
        tokb_sb = sb("tokb_sb", [TT, H])
        vb_sb = sb("vb_sb", [TT, H])
        qkb_sb = sb("qkb_sb", [HK, 4])
        nscale_sb = sb("nscale_sb", [TT, H])
        gateb_sb = sb("gateb_sb", [TT, E])
        ident = sb("ident", [128, 128])
        clip_mask = sb("clip_mask", [TT, TT])
        before = sb("before", [TT, SLOTS], F16)
        ones = sb("ones", [TT, SLOTS], F16)
        iota_e = sb("iota_e", [TT, E])
        iota_s = sb("iota_s", [TT, SLOTS], F16)
        token_id = sb("token_id", [TT, TILES])
        pad_row = sb("pad_row", [SLOTS, 2])
        lower = sb("lower", [E, TILES, E], F16)
        eps_sb = sb("eps_sb", [TT, 1])
        minus_half = sb("minus_half", [TT, 1])
        uc = sb("uc", [TT, 2, H])
        x_sb = sb("x_sb", [FK, RING * FC * TT])
        h = sb("h", [TT, TILES, H])
        hn_all = sb("hn_all", [128, TILES * H])
        hn = hn_all[0:TT, :].rearrange("p (i n) -> p i n", i=TILES)
        ln2_all = sb("ln2_all", [128, TILES * H])
        ln2 = ln2_all[0:TT, :].rearrange("p (i n) -> p i n", i=TILES)
        bn = sb("bn", [TT, TILES, 6])
        mv = sb("mv", [TT, TILES, 2])
        mv2 = sb("mv2", [TT, TILES, 2])
        var_eps = sb("var_eps", [TT, TILES])
        rstd = sb("rstd", [TT, TILES])
        var2 = sb("var2", [TT, TILES, 2])
        rstd2 = sb("rstd2", [TT, TILES, 2])
        hT = sb("hT", [HK, 2, HC, TT])
        tT = sb("tT", [HK, 2, HC, TT])
        key_all = sb("key_all", [128, 2 * HC * TT])
        key = key_all[0:HK, :].rearrange("p (b m t) -> p b m t", b=2, m=HC)
        fold = sb("fold", [HK, HC, H])
        fold_k = sb("fold_k", [HK, HC])
        fold_q = qkvw_sb[:, :, 3 * H + 1]
        fold_1 = sb("fold_1", [TT, 1])
        int_sb = key_all[:, 0:3 * 160].bitcast(I32).rearrange("p (a n) -> p a n", a=3)
        v = sb("v", [TT, 2, H + 1])
        sm = sb("sm", [TT, TT])
        nmax = sb("nmax", [TT, TILES])
        prob = sb("prob", [TT, TT])
        psums = sb("psums", [TT, TILES])
        rsum = sb("rsum", [TT, TILES])
        probT = sb("probT", [TT, TT])
        logits = sb("logits", [TT, TILES, E])
        top = sb("top", [TT, TILES, 8])
        topi = sb("topi", [TT, TILES, 8], U32)
        topif = sb("topif", [TT, TILES, K])
        nh = TILES * K * E
        hot = tokw[0:TT, 0:nh].rearrange("p (i k e) -> p i k e", i=TILES, k=K)
        prod = tokw[0:TT, nh:2 * nh].rearrange("p (i k e) -> p i k e", i=TILES, k=K)
        hot3 = tokw[0:TT, 0:nh].rearrange("p (c e) -> p c e", e=E)
        prod3 = tokw[0:TT, nh:2 * nh].rearrange("p (c e) -> p c e", e=E)
        mask = sb("mask", [TT, TILES, E], F16)
        dv = sb("dv", [TT, TILES, K])
        ev = sb("ev", [TT, TILES, K])
        es = sb("es", [TT, TILES])
        route = sb("route", [TT, TILES, K])
        comb = sb("comb", [TT, TILES, E])
        comb_prod = qkvw[0:TT, 0:K * TILES * E].rearrange("p (k i e) -> p k i e", k=K, i=TILES)
        combT = sb("combT", [E, TILES, TT])
        cnt_i = tokw[0:E, 2 * nh:2 * nh + 2 * TT].bitcast(I32).rearrange("p (a t) -> p a t", a=2)
        cnt_t = sb("cnt_t", [E, TT], F16)
        cnt_c = sb("cnt_c", [E, 1])
        upto = sb("upto", [E, E], F16)
        iota_c = sb("iota_c", [E, MT])
        ended = sb("ended", [E, MT], F16)
        o = K * TILES * E
        pos_i = qkvw[0:TT, o:o + 3 * PAIRS].bitcast(I32).rearrange("p (a c) -> p a c", a=3)
        pos_lo = qkvw[0:TT, o + 3 * PAIRS:o + 4 * PAIRS]
        pos_hi = qkvw[0:TT, o + 4 * PAIRS:o + 5 * PAIRS].bitcast(F16)[:, 0:PAIRS]
        owner = sb("owner", [1, MT], I32)
        pad_now = sb("pad_now", [SLOTS, MT])
        get_row = sb("get_row", [SLOTS, MT], U32)
        put_row = sb("put_row", [SLOTS, MT], U32)
        xg = [hn_all[:, c * ROW:(c + 1) * ROW] for c in range(RING)]
        ysb = [hn_all[:, RING * ROW + c * H:RING * ROW + (c + 1) * H] for c in range(RING)]
        weight = sb("weight", [SLOTS, RING])
        xT = sb("xT", [HK + 1, 2, HC, SLOTS])
        glu, lin, sig, gs = (ln2_all[:, n * I:(n + 1) * I] for n in range(4))
        act_a = tokw[:, 2 * nh:2 * nh + I]
        aT = tokw[:, 2 * nh + I:2 * nh + 2 * I].rearrange("p (c t) -> p c t", c=IC)

        x_ring = x_sb[:, :].rearrange("p (r c t) -> p r c t", r=RING, c=FC)
        half = x_sb[:, :].bitcast(F16)
        nl = PAIRS * SLOTS
        nr = PAIRS * MT
        lo_hot = half[:, 0:nl].rearrange("p (c s) -> p c s", c=PAIRS)
        hi_val = half[:, nl:nl + 2 * nr].rearrange("p (c v m) -> p c v m", c=PAIRS, v=2)

        bank = [ctx.enter_context(nc.psum_tensor(f"bank{n}", [128, 512], F32)) for n in range(8)]
        ps_emb = [bank[int(i == 1)][0:TT, 0:H] for i in range(TILES)]
        ps_hT = bank[2][0:HK, 0:HC * TT].rearrange("p (c t) -> p c t", c=HC)
        o = HC * (H + 1)
        ps_fold = bank[3][0:HK, 0:o].rearrange("p (c n) -> p c n", c=HC)
        ps_fold_k = bank[3][0:HK, o:o + HC]
        ps_fold_1 = bank[3][0:TT, o + HC:o + HC + 1]
        ps_key = bank[3][0:HK, 0:HC * TT].rearrange("p (c t) -> p c t", c=HC)
        ps_v = bank[4][0:TT, 0:H + 1]
        ps_s = bank[5][0:TT, 0:TT]
        ps_pT = bank[6][0:TT, 0:TT]
        ps_o = bank[7][0:TT, 0:H]
        late = [bank[int(i < TILES - 1)] for i in range(TILES)]
        ps_tT = [late[i][0:HK, 0:HC * TT].rearrange("p (c t) -> p c t", c=HC) for i in range(TILES)]
        ps_gate = [late[i][0:TT, HC * TT:HC * TT + E] for i in range(TILES)]
        ps_end = bank[7][0:E, 0:1]
        ps_owner = bank[7][0:1, 1:1 + MT]
        ps_rank = bank[4][0:TT, 0:TILES * E]
        ps_cnt = bank[5][0:E, 0:TT]
        ps_rows = bank[6][0:SLOTS, 0:2 * MT]
        ps_cT = [bank[n][0:E, 0:4 * TT].rearrange("p (c t) -> p c t", c=4) for n in (0, 1)]
        ps_b2 = [bank[n][0:TT, 0:2 * H].rearrange("p (c t) -> p c t", c=2) for n in (3, 2, 4, 5)]
        ps_glu = bank[0][:, 0:I]
        ps_lin = bank[1][:, 0:I]
        ps_aT = bank[2][:, 0:IC * SLOTS].rearrange("p (c t) -> p c t", c=IC)
        ps_xT = bank[3][0:HK, 0:HC * SLOTS].rearrange("p (c t) -> p c t", c=HC)
        ps_y = bank[4][:, 0:H]

        s_x = [sem(f"s_x{c}") for c in range(RING)]
        s_first = [sem(f"s_first{n}") for n in range(len(FIRST) - 1)]
        s_small = sem("s_small")
        s_qkvw = sem("s_qkvw")
        s_w1 = sem("s_w1")
        s_w2 = sem("s_w2")
        N_SMALL = 6
        s_tokb = sem("s_tokb")
        s_pool = sem("s_pool")
        s_const = sem("s_const")
        s_iotas = sem("s_iotas")
        s_emb = sem("s_emb")
        s_h = sem("s_h")
        s_stat = sem("s_stat")
        s_rstd = sem("s_rstd")
        s_hn = sem("s_hn")
        s_hT = sem("s_hT")
        s_hTc = sem("s_hTc")
        s_fold = sem("s_fold")
        s_foldc = sem("s_foldc")
        s_mask_c = sem("s_mask_c")
        s_key = sem("s_key")
        s_v = sem("s_v")
        s_keyc = sem("s_keyc")
        s_vc = sem("s_vc")
        s_s = sem("s_s")
        s_sm = sem("s_sm")
        s_nmax = sem("s_nmax")
        s_prob = sem("s_prob")
        s_pT = sem("s_pT")
        s_pTc = sem("s_pTc")
        s_o = sem("s_o")
        s_h2 = sem("s_h2")
        s_stat2 = sem("s_stat2")
        s_rstd2 = sem("s_rstd2")
        s_rms = sem("s_rms")
        s_vb = sem("s_vb")
        s_u = sem("s_u")
        s_t = sem("s_t")
        s_trow = sem("s_trow")
        s_tT = sem("s_tT")
        s_tTc = sem("s_tTc")
        s_gate = sem("s_gate")
        s_logit = sem("s_logit")
        s_top = sem("s_top")
        s_topi = sem("s_topi")
        s_rsum = sem("s_rsum")
        s_bn = sem("s_bn")
        s_dve = sem("s_dve")
        s_mask = sem("s_mask")
        s_rank = sem("s_rank")
        s_dv = sem("s_dv")
        s_ev = sem("s_ev")
        s_route = sem("s_route")
        s_comb = sem("s_comb")
        s_cT = sem("s_cT")
        s_cTc = sem("s_cTc")
        s_b2 = sem("s_b2")
        s_b2c = sem("s_b2c")
        s_cntc = sem("s_cntc")
        s_cnt = sem("s_cnt")
        s_end = sem("s_end")
        s_ended = sem("s_ended")
        s_own = sem("s_own")
        s_owner = sem("s_owner")
        s_pos = sem("s_pos")
        s_hi = sem("s_hi")
        s_hi_val = sem("s_hi_val")
        s_hot = sem("s_hot")
        s_hot_pool = sem("s_hot_pool")
        s_rows = sem("s_rows")
        s_table = sem("s_table")
        s_base = sem("s_base")
        s_got = [sem(f"s_got{c}") for c in range(RING)]
        s_put = sem("s_put")
        s_base_out = sem("s_base_out")
        s_weight = sem("s_weight")
        s_xT = sem("s_xT")
        s_xTc = sem("s_xTc")
        s_glu = sem("s_glu")
        s_gluc = sem("s_gluc")
        s_sig = sem("s_sig")
        s_lin = sem("s_lin")
        s_linc = sem("s_linc")
        s_gs = sem("s_gs")
        s_a = sem("s_a")
        s_aT = sem("s_aT")
        s_aTc = sem("s_aTc")
        s_y = sem("s_y")
        s_yc = sem("s_yc")
        def wait(eng, s, value):
            if not isinstance(value, int) or value > 0:
                eng.wait_ge(s, value)

        def slot_steps(eng, step):
            whole = (MT - 2) // UNROLL
            for c in range(UNROLL + 1):
                step(0, c)
            with eng.Fori(1, whole) as g:
                for c in range(1, UNROLL + 1):
                    step(g, c)
            for c in range(1, MT - UNROLL * whole):
                step(whole, c)

        block = ctx.enter_context(nc.Block())

        @block.sync
        def _(sp):
            for n in range(len(FIRST) - 1):
                c = slice(FIRST[n], FIRST[n + 1])
                sp.dma_start(tokw_sb[:, c, :], tok_w[:, c, :]).then_inc(s_first[n], 16)
                sp.dma_start(x_ring[:, 0, c], x[0][:, c, :]).then_inc(s_first[n], 16)
            def load_expert(e):
                sp.dma_start(w1_sb[0:HK, e * W1E:(e + 1) * W1E], w1[e]).then_inc(s_w1, 16)
                sp.dma_start(w2_sb[:, e * W2E:(e + 1) * W2E], w2[e]).then_inc(s_w2, 16)

            for i in range(1, TILES):
                if i >= RING:
                    sp.wait_ge(s_emb, i - RING + 1)
                sp.dma_start(x_ring[:, i % RING], x[i]).then_inc(s_x[i % RING], 16)
                if i == 1:
                    sp.dma_start(tokb_sb[:, :], tok_b.broadcast_to([TT, H])).then_inc(s_tokb, 16)
                if i == RING - 1:
                    sp.dma_start(vb_sb[:, :], v_b.broadcast_to([TT, H])).then_inc(s_small, 16)
                    sp.dma_start(nscale_sb[:, :], norm_scale.broadcast_to([TT, H])).then_inc(s_small, 16)
                    sp.dma_start(gateb_sb[:, :], gate_b.broadcast_to([TT, E])).then_inc(s_small, 16)
                    sp.dma_start(qkb_sb[:, :], qk_b).then_inc(s_small, 16)
                    sp.dma_start(gatew_sb[:, :, :], gate_w).then_inc(s_small, 16)
                    sp.dma_start(b2_sb[:, :], b2).then_inc(s_small, 16)
                    sp.dma_start(qkvw_sb[:, :, 0:3 * H + 1], qkv_w).then_inc(s_qkvw, 16)
                    sp.dma_start(w1_sb[HK:HK + 1, :].rearrange("p (e c n) -> p e c n", e=E, c=HC)[:, :, HC - 1, :],
                                 b1).then_inc(s_w1, 16)
                if i >= RING:
                    for e in range(2 * (i - RING), 2 * (i - RING) + 2):
                        load_expert(e)
            for e in range(2 * (TILES - RING), E):
                load_expert(e)
            for i in range(TILES):
                sp.wait_ge(s_t, i + 1)
                sp.dma_start(t_rows[i * TT:(i + 1) * TT, 0:H], hn[:, i, :]).then_inc(s_trow, 16)
            sp.wait_ge(s_w2, 16 * E)
            sp.dma_start(out[TOKENS:TOKENS + SLOTS, :], w2_sb[:, 0:H]).then_inc(s_base_out, 16)
            sp.wait_ge(s_comb, 1)
            sp.dma_start(t_rows.rearrange("(i p) n -> p i n", p=TT)[:, :, H:ROW], comb[:, :, :]).then_inc(s_trow, 16)
            sp.wait_ge(s_b2c, 4)
            sp.dma_start(out[0:TOKENS, :].rearrange("(i p) n -> p i n", p=TT), h[:, :, :]).then_inc(s_base_out, 16)
            sp.wait_ge(s_base_out, 32)
            sp.wait_ge(s_put, 16 * MT)

        @block.gpsimd
        def _(pool):
            n = 0

            def link(ins):
                nonlocal n
                n += 1
                ins.then_inc(s_pool, 1)
                pool.wait_ge(s_pool, n)

            g = nc.gpsimd
            link(g.memset(eps_sb[:, :], EPS))
            link(g.memset(minus_half[:, :], -0.5))
            link(g.memset(ident[:, :], 0.0))
            g.affine_select(out=ident[:, :], in_=ident[:, :], compare_op=ALU.not_equal, fill=1.0, base=0,
                            pattern=[[-1, 128]], channel_multiplier=1).then_inc(s_const, 1)
            link(g.memset(clip_mask[:, :], 0.0))
            cm = clip_mask[:, :].rearrange("p (b w) -> p b w", w=SEQ)
            link(g.affine_select(out=cm, in_=cm, compare_op=ALU.is_ge, fill=OFF_CLIP, base=0,
                                 pattern=[[-SEQ, TT // SEQ], [0, SEQ]], channel_multiplier=1))
            g.affine_select(out=cm, in_=cm, compare_op=ALU.is_ge, fill=OFF_CLIP, base=SEQ - 1,
                            pattern=[[SEQ, TT // SEQ], [0, SEQ]], channel_multiplier=-1).then_inc(s_const, 1)
            g.memset(ones[:, :], 1.0).then_inc(s_const, 1)
            link(g.memset(before[:, :], 1.0))
            g.affine_select(out=before[:, :], in_=before[:, :], compare_op=ALU.is_ge, fill=0.0, base=-1,
                            pattern=[[1, SLOTS]], channel_multiplier=-1).then_inc(s_const, 1)
            link(g.memset(lower[:, :, :], float(SLOTS)))
            g.affine_select(out=lower[:, :, :], in_=lower[:, :, :], compare_op=ALU.is_ge, fill=0.0, base=-1,
                            pattern=[[0, TILES], [1, E]], channel_multiplier=-1).then_inc(s_const, 1)
            link(g.memset(upto[:, :], 1.0))
            g.affine_select(out=upto[:, :], in_=upto[:, :], compare_op=ALU.is_ge, fill=0.0, base=0,
                            pattern=[[1, E]], channel_multiplier=-1).then_inc(s_const, 1)
            pool.wait_ge(s_const, 6)
            g.memset(xT[HK:HK + 1, :, :, :], 1.0).then_inc(s_const, 1)
            pool.wait_ge(s_const, 7)
            g.iota(int_sb[:, 0, :], pattern=[[1, 160]], base=0, channel_multiplier=0).then_inc(s_iotas, 1)
            g.iota(int_sb[:, 1, 0:TILES], pattern=[[TT, TILES]], base=0, channel_multiplier=1).then_inc(s_iotas, 1)
            g.iota(int_sb[:, 2, 0:1], pattern=[[1, 1]], base=TOKENS, channel_multiplier=1).then_inc(s_iotas, 1)

            def root(i):
                pool.wait_ge(s_stat, i + 1)
                link(g.tensor_tensor(var_eps[:, i:i + 1], mv[:, i, 1:2], eps_sb[:, :], ALU.add))
                g.tensor_tensor(rstd[:, i:i + 1], var_eps[:, i:i + 1], minus_half[:, 0:1], ALU.pow).then_inc(s_rstd, 1)

            def v_bias(i):
                pool.wait_ge(s_hn, i + 1)
                g.tensor_tensor(h[:, i, :], h[:, i, :], vb_sb[:, :], ALU.add).then_inc(s_vb, 1)

            def root2(i):
                pool.wait_ge(s_stat2, i + 1)
                link(g.tensor_scalar(var2[:, i, 1:2], mv2[:, i, 1:2], 1.0 + EPS, EPS * EPS, ALU.mult, ALU.add))
                g.tensor_tensor(rstd2[:, i, 1:2], var2[:, i, 1:2], minus_half[:, 0:1], ALU.pow).then_inc(s_rms, 1)
                link(g.tensor_tensor(var2[:, i, 0:1], mv2[:, i, 1:2], eps_sb[:, :], ALU.add))
                g.tensor_tensor(rstd2[:, i, 0:1], var2[:, i, 0:1], minus_half[:, 0:1], ALU.pow).then_inc(s_rstd2, 1)

            def add_norm2(i):
                pool.wait_ge(s_rstd2, i + 1)
                link(g.tensor_scalar(ln2[:, i, :], h[:, i, :], mv2[:, i, 0:1], rstd2[:, i, 0:1],
                                     ALU.subtract, ALU.mult))
                pool.wait_ge(s_u, i + 1)
                g.tensor_tensor(h[:, i, :], h[:, i, :], ln2[:, i, :], ALU.add).then_inc(s_base, 1)

            pool.wait_ge(s_small, 16 * N_SMALL)
            for i in range(AHEAD):
                root(i)
                v_bias(i)
            for i in range(TILES + 2):
                if i >= 2:
                    root2(i - 2)
                if i + AHEAD < TILES:
                    root(i + AHEAD)
                if 2 <= i < TILES:
                    add_norm2(i - 2)
                if i + AHEAD < TILES:
                    v_bias(i + AHEAD)
            for i in range(TILES - 2, TILES):
                add_norm2(i)
            pool.wait_ge(s_route, 1)
            for k in range(K):
                ins = g.tensor_tensor(comb_prod[:, k], hot[:, :, k, :],
                                      route[:, :, k].unsqueeze(2).to_broadcast([TT, TILES, E]), ALU.mult)
            link(ins)
            link(g.tensor_tensor(comb_prod[:, 0:2], comb_prod[:, 0:2], comb_prod[:, 2:4], ALU.add))
            g.tensor_tensor(comb[:, :, :], comb_prod[:, 0], comb_prod[:, 1], ALU.add).then_inc(s_comb, 1)
            pool.wait_ge(s_pos, 1)
            for c in range(POOL_EVERY - 1, PAIRS, POOL_EVERY):
                g.tensor_scalar(lo_hot[:, c, :], iota_s[:, :], pos_lo[:, c:c + 1], None,
                                ALU.is_equal).then_inc(s_hot_pool, 1)

            def gather(m, slot):
                g.indirect_dma_start(out=xg[slot], out_offset=None, in_=t_rows,
                                     in_offset=bass.IndirectOffsetOnAxis(ap=get_row[:, m:m + 1], axis=0),
                                     ).then_inc(s_got[slot], 16)

            def scatter(m, slot):
                if m > 0:
                    pool.wait_ge(s_put, 16 * m)
                g.indirect_dma_start(out=out,
                                     out_offset=bass.IndirectOffsetOnAxis(ap=put_row[:, m:m + 1], axis=0),
                                     in_=ysb[slot], in_offset=None, compute_op=ALU.add,
                                     ).then_inc(s_put, 16)

            pool.wait_ge(s_table, 1)
            pool.wait_ge(s_trow, 16 * (TILES + 1))
            for m in range(2):
                gather(m, m)

            for j in range(MT):
                if j + 2 < MT:
                    if j > 0:
                        pool.wait_ge(s_xT, j)
                        pool.wait_ge(s_weight, j)
                    gather(j + 2, (j + 2) % RING)
                if j > 0:
                    if j == 1:
                        pool.wait_ge(s_table, 2)
                        pool.wait_ge(s_base_out, 32)
                    pool.wait_ge(s_yc, j)
                    scatter(j - 1, (j - 1) % RING)
            pool.wait_ge(s_yc, MT)
            scatter(MT - 1, (MT - 1) % RING)

        @block.scalar
        def _(act):
            a = nc.scalar
            def copy_hT(i):
                act.wait_ge(s_hT, i + 1)
                if i >= 2:
                    act.wait_ge(s_v, i - 1)
                    act.wait_ge(s_s, i - 1)
                a.copy(hT[:, i % 2], ps_hT).then_inc(s_hTc, 1)

            def softmax(i):
                act.wait_ge(s_nmax, i + 1)
                if i >= 1:
                    act.wait_ge(s_pT, i)
                a.activation(prob[:, :], sm[:, :], ACT.Exp, bias=nmax[:, i:i + 1],
                             accum_out=psums[:, i:i + 1]).then_inc(s_prob, 1)

            def copy_pT(i):
                act.wait_ge(s_pT, i + 1)
                if i >= 1:
                    act.wait_ge(s_o, i)
                a.copy(probT[:, :], ps_pT).then_inc(s_pTc, 1)

            def copy_v(i):
                act.wait_ge(s_v, i + 1)
                if i >= 2:
                    act.wait_ge(s_o, i - 1)
                a.copy(v[:, i % 2, :], ps_v).then_inc(s_vc, 1)

            def copy_tT(i):
                act.wait_ge(s_tT, i + 1)
                if i >= 2:
                    act.wait_ge(s_gate, i - 1)
                a.copy(tT[:, i % 2], ps_tT[i]).then_inc(s_tTc, 1)

            act.wait_ge(s_fold, 1)
            a.copy(fold[:, :, :], ps_fold[:, :, 0:H]).then_inc(s_foldc, 1)
            a.activation(fold_k[:, :], ps_fold_k, ACT.Copy, scale=SCALE).then_inc(s_foldc, 1)
            a.activation(fold_q, ps_fold[:, :, H], ACT.Copy, scale=SCALE).then_inc(s_foldc, 1)
            a.activation(fold_1[:, :], ps_fold_1, ACT.Copy, scale=SCALE).then_inc(s_foldc, 1)
            copy_hT(0)
            for i in range(TILES + 3):
                if 1 <= i <= TILES:
                    softmax(i - 1)
                    copy_pT(i - 1)
                if i >= 3:
                    copy_tT(i - 3)
                if i < TILES:
                    copy_v(i)
                if i + 1 < TILES:
                    copy_hT(i + 1)
            act.wait_ge(s_dv, 1)
            a.activation(ev[:, :, :], dv[:, :, :], ACT.Exp).then_inc(s_ev, 1)
            for n in range(2):
                act.wait_ge(s_cT, n + 1)
                a.copy(combT[:, 4 * n:4 * n + 4, :], ps_cT[n]).then_inc(s_cTc, 1)

            act.wait_ge(s_hi, 1)
            for i in range(TILES):
                c = slice(K * i, K * i + K)
                a.activation(hi_val[:, c, 0, :], hi_val[:, c, 1, :], ACT.Copy,
                             scale=token_id[:, i:i + 1]).then_inc(s_hi_val, 1)
            a.activation(sig[:, 0:1], pad_row[:, 0:1], ACT.Sigmoid)
            act.wait_ge(s_owner, 1)

            def copy_xT(j, slot, buf):
                act.wait_ge(s_xT, j + 1)
                wait(act, s_lin, j - 1)
                a.copy(xT[0:HK, buf], ps_xT).then_inc(s_xTc, 1)
                e = act.value_load(owner[0:1, bass.ds(j, 1) if not isinstance(j, int) else slice(j, j + 1)],
                                   min_val=0, max_val=E - 1)
                wait(act, s_yc, j + 1 - RING)
                a.copy(weight[:, slot:slot + 1], xg[slot][:, bass.ds(e + H, 1)]).then_inc(s_weight, 1)

            def copy_aT(j):
                act.wait_ge(s_aT, j + 1)
                wait(act, s_y, j)
                a.copy(aT[:, :, :], ps_aT).then_inc(s_aTc, 1)

            def copy_y(j, slot):
                act.wait_ge(s_y, j + 1)
                wait(act, s_put, 16 * (j + 1 - RING))
                act.wait_ge(s_weight, j + 1)
                a.activation(ysb[slot], ps_y, ACT.Copy, scale=weight[:, slot:slot + 1]).then_inc(s_yc, 1)

            copy_xT(0, 0, 0)

            def step(gi, c):
                j = UNROLL * gi + c
                first = isinstance(j, int) and j == 0
                if not first:
                    copy_aT(j - 1)
                act.wait_ge(s_gluc, j + 1)
                wait(act, s_gs, j)
                a.activation(sig, glu, ACT.Sigmoid, scale=ALPHA).then_inc(s_sig, 1)
                if not (isinstance(j, int) and j == MT - 1):
                    copy_xT(j + 1, (c + 1) % RING, (c + 1) % 2)
                if not first:
                    copy_y(j - 1, (c - 1) % RING)

            slot_steps(act, step)
            copy_aT(MT - 1)
            copy_y(MT - 1, (MT - 1) % RING)

        @block.vector
        def _(dve):
            d = nc.vector
            n = 0

            def link(ins):
                nonlocal n
                n += 1
                ins.then_inc(s_dve, 1)
                dve.wait_ge(s_dve, n)

            dve.wait_ge(s_iotas, 3)
            d.tensor_copy(iota_e[:, :], int_sb[0:TT, 0, 0:E])
            d.tensor_copy(iota_s[:, :], int_sb[0:TT, 0, 0:SLOTS])
            d.tensor_copy(token_id[:, :], int_sb[0:TT, 1, 0:TILES])
            d.tensor_copy(iota_c[:, :], int_sb[0:E, 0, 0:MT])
            link(d.tensor_copy(pad_row[:, 0:1], int_sb[:, 2, 0:1]))
            d.tensor_scalar(pad_row[:, 1:2], pad_row[:, 0:1], -1.0, None, ALU.mult)

            dve.wait_ge(s_tokb, 16)

            def embed(i):
                dve.wait_ge(s_emb, i + 1)
                d.tensor_tensor(h[:, i, :], ps_emb[i], tokb_sb[:, :], ALU.add).then_inc(s_h, 1)
                dve.wait_ge(s_h, i + 1)
                link(d.bn_stats(bn[:, i, :], h[:, i, :]))
                d.bn_aggr(mv[:, i, :], bn[:, i, :]).then_inc(s_stat, 1)

            def normalise(i):
                dve.wait_ge(s_rstd, i + 1)
                d.tensor_scalar(hn[:, i, :], h[:, i, :], mv[:, i, 0:1], rstd[:, i:i + 1],
                                ALU.subtract, ALU.mult).then_inc(s_hn, 1)

            def scores(i):
                dve.wait_ge(s_s, i + 1)
                dve.wait_ge(s_vc, i + 1)
                if i >= 1:
                    dve.wait_ge(s_prob, i)
                d.scalar_tensor_tensor(out=sm[:, :], in0=ps_s, scalar=v[:, i % 2, H:H + 1], in1=clip_mask[:, :],
                                       op0=ALU.add, op1=ALU.add).then_inc(s_sm, 1)
                if i >= 1:
                    d.reciprocal(rsum[:, i - 1:i], psums[:, i - 1:i]).then_inc(s_rsum, 1)
                dve.wait_ge(s_sm, i + 1)
                d.tensor_reduce(nmax[:, i:i + 1], sm[:, :], AX.X, ALU.max, negate=True).then_inc(s_nmax, 1)

            def copy_key(i):
                dve.wait_ge(s_key, i + 1)
                if i >= 2:
                    dve.wait_ge(s_s, i - 1)
                d.scalar_tensor_tensor(out=key[:, i % 2], in0=ps_key, scalar=SCALE,
                                       in1=fold_k[:, :].unsqueeze(2).to_broadcast([HK, HC, TT]),
                                       op0=ALU.mult, op1=ALU.add).then_inc(s_keyc, 1)

            def add_gate_bias(j):
                dve.wait_ge(s_gate, j + 1)
                dve.wait_ge(s_rms, j + 1)
                d.scalar_tensor_tensor(out=logits[:, j, :], in0=ps_gate[j], scalar=rstd2[:, j, 1:2],
                                       in1=gateb_sb[:, :], op0=ALU.mult, op1=ALU.add).then_inc(s_logit, 1)

            def largest(j):
                dve.wait_ge(s_logit, j + 1)
                d.max(top[:, j, :], logits[:, j, :]).then_inc(s_top, 1)

            def their_experts(j):
                dve.wait_ge(s_top, j + 1)
                d.max_index(topi[:, j, :], top[:, j, :], logits[:, j, :]).then_inc(s_topi, 1)

            def residual_and_pick(i, j):
                dve.wait_ge(s_rsum, i + 1)
                dve.wait_ge(s_vb, i + 1)
                dve.wait_ge(s_o, i + 1)
                d.scalar_tensor_tensor(out=h[:, i, :], in0=ps_o, scalar=rsum[:, i:i + 1], in1=h[:, i, :],
                                       op0=ALU.mult, op1=ALU.add).then_inc(s_h2, 1)
                if j >= 0:
                    add_gate_bias(j)
                dve.wait_ge(s_h2, i + 1)
                d.bn_stats(bn[:, i, :], h[:, i, :]).then_inc(s_bn, 1)
                if j >= 0:
                    largest(j)
                dve.wait_ge(s_bn, i + 1)
                d.bn_aggr(mv2[:, i, :], bn[:, i, :]).then_inc(s_stat2, 1)
                if j >= 0:
                    their_experts(j)
                dve.wait_ge(s_stat2, i + 1)
                if i >= 2:
                    dve.wait_ge(s_t, i - 1)
                    dve.wait_ge(s_tT, i - 1)
                d.scalar_tensor_tensor(out=uc[:, i % 2, :], in0=h[:, i, :], scalar=mv2[:, i, 0:1],
                                       in1=nscale_sb[:, :], op0=ALU.subtract, op1=ALU.mult).then_inc(s_u, 1)

            def normalise2(i):
                dve.wait_ge(s_rms, i + 1)
                dve.wait_ge(s_u, i + 1)
                d.tensor_scalar(hn[:, i, :], uc[:, i % 2, :], rstd2[:, i, 1:2], None, ALU.mult).then_inc(s_t, 1)

            for i in range(AHEAD):
                embed(i)
                normalise(i)
            def hots(lo, hi):
                c = slice(K * lo, K * hi)
                link(d.tensor_copy(topif[:, lo:hi, :], topi[:, lo:hi, 0:K]))
                link(d.tensor_tensor(hot3[:, c], topif[:, lo:hi, :].rearrange("p i k -> p (i k)").unsqueeze(2)
                                     .to_broadcast([TT, K * (hi - lo), E]),
                                     iota_e[:, :].unsqueeze(1).to_broadcast([TT, K * (hi - lo), E]), ALU.is_equal))
                with nc.allow_low_precision("counts of 0 and 1 are exact"):
                    d.tensor_reduce(mask[:, lo:hi, :], hot[:, lo:hi, :, :].rearrange("p i k e -> p i e k"), AX.X,
                                    ALU.add).then_inc(s_mask, 1)

            dve.wait_ge(s_const, 2)
            dve.wait_ge(s_small, 16 * N_SMALL)
            dve.wait_ge(s_foldc, 4)
            d.tensor_scalar(clip_mask[:, :], clip_mask[:, :], fold_1[:, :], None, ALU.add).then_inc(s_mask_c, 1)
            dve.wait_ge(s_mask_c, 1)
            for i in range(TILES + 2):
                if 1 <= i <= TILES:
                    scores(i - 1)
                if i >= 2:
                    residual_and_pick(i - 2, i - 4)
                if i + AHEAD < TILES:
                    embed(i + AHEAD)
                if i < TILES:
                    copy_key(i)
                if i == TILES:
                    dve.wait_ge(s_prob, TILES)
                    d.reciprocal(rsum[:, i - 1:i], psums[:, i - 1:i]).then_inc(s_rsum, 1)
                if i == TILES + 1:
                    dve.wait_ge(s_topi, EARLY)
                    hots(0, EARLY)
                if 2 <= i < TILES + 1:
                    normalise2(i - 2)
                if i + AHEAD < TILES:
                    normalise(i + AHEAD)
            normalise2(TILES - 1)
            for step in (add_gate_bias, largest):
                step(TILES - 2)
                step(TILES - 1)
            dve.wait_ge(s_top, TILES)
            d.tensor_tensor(dv[:, :, :], top[:, :, 0:K], top[:, :, 0:1].to_broadcast([TT, TILES, K]),
                            ALU.subtract).then_inc(s_dv, 1)
            their_experts(TILES - 2)
            their_experts(TILES - 1)
            dve.wait_ge(s_topi, TILES)

            hots(EARLY, TILES)
            dve.wait_ge(s_ev, 1)
            link(d.tensor_reduce(es[:, :], ev[:, :, :], AX.X, ALU.add))
            link(d.reciprocal(es[:, :], es[:, :]))
            d.tensor_tensor(route[:, :, :], ev[:, :, :], es[:, :].unsqueeze(2).to_broadcast([TT, TILES, K]),
                            ALU.mult).then_inc(s_route, 1)
            dve.wait_ge(s_cnt, 1)
            link(d.tensor_scalar(cnt_i[:, 0, :], ps_cnt, float(SLOTS - 1), None, ALU.add))
            link(d.tensor_scalar(cnt_i[:, 1, :], cnt_i[:, 0, :], SLOT_BITS, None, ALU.arith_shift_right))
            d.tensor_copy(cnt_t[:, :], cnt_i[:, 1, :]).then_inc(s_cntc, 1)
            dve.wait_ge(s_rank, 1)
            link(d.tensor_tensor(prod, hot, ps_rank.rearrange("p (i e) -> p i e", e=E).unsqueeze(2)
                                 .to_broadcast([TT, TILES, K, E]), ALU.mult))
            with nc.allow_low_precision("whole numbers"):
                link(d.tensor_reduce(pos_i[:, 0, :], prod3, AX.X, ALU.add))
            d.tensor_scalar(pos_i[:, 1, :], pos_i[:, 0, :], SLOTS - 1, None, ALU.bitwise_and)
            link(d.tensor_scalar(pos_i[:, 2, :], pos_i[:, 0, :], SLOT_BITS, None, ALU.arith_shift_right))
            d.tensor_copy(pos_lo, pos_i[:, 1, :]).then_inc(s_pos, 1)
            link(d.tensor_copy(pos_hi, pos_i[:, 2, :]))
            d.tensor_tensor(hi_val[:, :, 1, :], pos_hi.unsqueeze(2).to_broadcast([TT, PAIRS, MT]),
                            iota_s[:, 0:MT].unsqueeze(1).to_broadcast([TT, PAIRS, MT]),
                            ALU.is_equal).then_inc(s_hi, 1)
            dve.wait_ge(s_end, 1)
            link(d.tensor_copy(cnt_c[:, :], ps_end))
            d.tensor_scalar(ended[:, :], iota_c[:, :], cnt_c[:, 0:1], None, ALU.is_ge).then_inc(s_ended, 1)
            for c in [c for c in range(PAIRS) if c % POOL_EVERY < POOL_EVERY - 1]:
                d.tensor_scalar(lo_hot[:, c, :], iota_s[:, :], pos_lo[:, c:c + 1], None,
                                ALU.is_equal).then_inc(s_hot, 1)
            dve.wait_ge(s_own, 1)
            d.tensor_scalar(owner[:, :], ps_owner, float(E - 1), None, ALU.min).then_inc(s_owner, 1)
            dve.wait_ge(s_rows, 1)
            d.tensor_copy(get_row[:, :], ps_rows[:, 0:MT]).then_inc(s_table, 1)
            link(d.tensor_scalar(pad_now[:, :], ps_rows[:, MT:2 * MT], pad_row[:, 1:2], pad_row[:, 0:1],
                                 ALU.mult, ALU.add))
            d.tensor_tensor(put_row[:, :], pad_now[:, :], ps_rows[:, 0:MT], ALU.add).then_inc(s_table, 1)
            dve.wait_ge(s_base, TILES)
            for q in range(4):
                dve.wait_ge(s_b2, q + 1)
                d.tensor_tensor(h[:, 2 * q:2 * q + 2, :], h[:, 2 * q:2 * q + 2, :], ps_b2[q],
                                ALU.add).then_inc(s_b2c, 1)

            def step(gi, c):
                j = UNROLL * gi + c
                dve.wait_ge(s_glu, j + 1)
                wait(dve, s_gs, j)
                d.tensor_scalar(glu, ps_glu, LIMIT, None, ALU.min).then_inc(s_gluc, 1)
                dve.wait_ge(s_sig, j + 1)
                wait(dve, s_a, j)
                d.tensor_tensor(gs, glu, sig, ALU.mult).then_inc(s_gs, 1)
                dve.wait_ge(s_lin, j + 1)
                d.tensor_scalar(lin, ps_lin, LIMIT, -LIMIT, ALU.min, ALU.max).then_inc(s_linc, 1)
                dve.wait_ge(s_linc, j + 1)
                dve.wait_ge(s_gs, j + 1)
                wait(dve, s_aT, j)
                d.scalar_tensor_tensor(out=act_a, in0=lin, scalar=1.0, in1=gs,
                                       op0=ALU.add, op1=ALU.mult).then_inc(s_a, 1)

            slot_steps(dve, step)

        @block.tensor
        def _(pe):
            t = nc.tensor

            def turn_h(i):
                pe.wait_ge(s_hn, i + 1)
                if i >= 1:
                    pe.wait_ge(s_hTc, i)
                for c in range(HC):
                    ins = t.transpose(ps_hT[:, c, :], hn[:, i, c * HK:(c + 1) * HK], ident[0:TT, 0:TT])
                ins.then_inc(s_hT, 1)

            def embed(i):
                if i >= 1:
                    pe.wait_ge(s_x[i % RING], 16 * (i // RING + (i % RING > 0)))
                if i >= 2:
                    pe.wait_ge(s_h, i if i > 2 else 1)
                for c in range(FC):
                    if i == 0 and c in FIRST:
                        pe.wait_ge(s_first[FIRST.index(c)], 32)
                    ins = t.matmul(ps_emb[i], x_ring[:, i % RING, c, :], tokw_sb[:, c, :],
                                   start=(c == 0), stop=(c == FC - 1))
                ins.then_inc(s_emb, 1)

            def fold_weights():
                def product(dst, lhs, rhs):
                    for c in range(HC):
                        ins = t.matmul(dst, lhs(c), rhs(c), start=(c == 0), stop=(c == HC - 1))
                    return ins

                for m in range(HC):
                    wq = lambda c: qkvw_sb[:, c, m * HK:(m + 1) * HK]
                    wk = lambda c: qkvw_sb[:, c, H + m * HK:H + (m + 1) * HK]
                    product(ps_fold[:, m, :], wq, lambda c: qkvw_sb[:, c, H:2 * H + 1])
                    product(ps_fold_k[:, m:m + 1], wk, lambda c: qkb_sb[:, c:c + 1])
                product(ps_fold_1, lambda c: qkb_sb[:, c:c + 1].to_broadcast([HK, TT]),
                        lambda c: qkb_sb[:, HC + c:HC + c + 1]).then_inc(s_fold, 1)

            def keys(i):
                pe.wait_ge(s_hTc, i + 1)
                if i == 0:
                    pe.wait_ge(s_foldc, 4)
                if i >= 1:
                    pe.wait_ge(s_keyc, i)
                for m in range(HC):
                    for c in range(HC):
                        ins = t.matmul(ps_key[:, m, :], fold[:, c, m * HK:(m + 1) * HK], hT[:, i % 2, c, :],
                                       start=(c == 0), stop=(c == HC - 1))
                ins.then_inc(s_key, 1)

            def value(i):
                if i >= 1:
                    pe.wait_ge(s_vc, i)
                for c in range(HC):
                    ins = t.matmul(ps_v, hT[:, i % 2, c, :], qkvw_sb[:, c, 2 * H + 1:3 * H + 2],
                                   start=(c == 0), stop=(c == HC - 1))
                ins.then_inc(s_v, 1)

            def score(i):
                pe.wait_ge(s_keyc, i + 1)
                if i >= 1:
                    pe.wait_ge(s_sm, i)
                for c in range(HC):
                    ins = t.matmul(ps_s, key[:, i % 2, c, :], hT[:, i % 2, c, :],
                                   start=(c == 0), stop=(c == HC - 1))
                ins.then_inc(s_s, 1)

            def turn_p(i):
                pe.wait_ge(s_prob, i + 1)
                if i >= 1:
                    pe.wait_ge(s_pTc, i)
                t.transpose(ps_pT, prob[:, :], ident[0:TT, 0:TT]).then_inc(s_pT, 1)

            def context(i):
                pe.wait_ge(s_pTc, i + 1)
                pe.wait_ge(s_vc, i + 1)
                if i >= 1:
                    pe.wait_ge(s_h2, i)
                t.matmul(ps_o, probT[:, :], v[:, i % 2, 0:H], start=True, stop=True).then_inc(s_o, 1)

            def turn_t(i):
                pe.wait_ge(s_u, i + 1)
                if 1 <= i < TILES - 1:
                    pe.wait_ge(s_logit, i)
                if i == TILES - 1:
                    pe.wait_ge(s_h, TILES)
                for c in range(HC):
                    ins = t.transpose(ps_tT[i][:, c, :], uc[:, i % 2, c * HK:(c + 1) * HK], ident[0:TT, 0:TT])
                ins.then_inc(s_tT, 1)

            def gate(i):
                pe.wait_ge(s_tTc, i + 1)
                for c in range(HC):
                    ins = t.matmul(ps_gate[i], tT[:, i % 2, c, :], gatew_sb[:, c, :],
                                   start=(c == 0), stop=(c == HC - 1))
                ins.then_inc(s_gate, 1)

            def count(lo, hi):
                for i in range(lo, hi):
                    ins = t.matmul(ps_cnt, mask[:, i, :], ones[:, 0:TT], start=(i == 0), stop=(i == TILES - 1))
                return ins

            for i in range(AHEAD):
                embed(i)
            pe.wait_ge(s_small, 16 * N_SMALL)
            pe.wait_ge(s_qkvw, 16)
            fold_weights()
            pe.wait_ge(s_const, 7)
            turn_h(0)
            for i in range(TILES + 2):
                if 1 <= i <= TILES:
                    score(i - 1)
                if i + AHEAD < TILES:
                    embed(i + AHEAD)
                if i < TILES:
                    keys(i)
                if 1 <= i <= TILES:
                    turn_p(i - 1)
                if i >= 3:
                    turn_t(i - 3)
                if i < TILES:
                    value(i)
                if 1 <= i <= TILES:
                    context(i - 1)
                if i + 1 < TILES:
                    turn_h(i + 1)
                if i == TILES + 1:
                    turn_t(TILES - 1)
                if i >= 3:
                    gate(i - 3)
            gate(TILES - 1)
            pe.wait_ge(s_mask, 1)
            count(0, EARLY)

            pe.wait_ge(s_mask, 2)
            count(EARLY, TILES).then_inc(s_cnt, 1)
            m2 = mask[:, :, :].rearrange("p i e -> p (i e)")
            t.matmul(ps_rank, before[:, 0:TT], m2, start=True, stop=False)
            for s in range(1, TILES):
                t.matmul(ps_rank[:, s * E:TILES * E], ones[:, 0:TT], m2[:, 0:(TILES - s) * E],
                         start=False, stop=False)
            pe.wait_ge(s_cntc, 1)
            t.matmul(ps_rank, cnt_t[:, :], lower[:, :, :].rearrange("p i e -> p (i e)"),
                     start=False, stop=True).then_inc(s_rank, 1)
            t.matmul(ps_end, upto[:, :], cnt_t[:, 0:1], start=True, stop=True).then_inc(s_end, 1)
            pe.wait_ge(s_comb, 1)
            pe.wait_ge(s_logit, TILES)
            for n in range(2):
                for i in range(4):
                    ins = t.transpose(ps_cT[n][:, i, :], comb[:, 4 * n + i, :], ident[0:TT, 0:TT])
                ins.then_inc(s_cT, 1)

            def bias2(q):
                pe.wait_ge(s_cTc, q // 2 + 1)
                for i in range(2):
                    ins = t.matmul(ps_b2[q][:, i, :], combT[:, 2 * q + i, :], b2_sb[:, :],
                                   start=True, stop=True)
                ins.then_inc(s_b2, 1)

            bias2(0)
            pe.wait_ge(s_ended, 1)
            t.matmul(ps_owner, ones[0:E, 0:1], ended[:, :], start=True, stop=True).then_inc(s_own, 1)
            for c in range(PAIRS):
                if c % K == 0:
                    by_pool = (c + K) // POOL_EVERY
                    pe.wait_ge(s_hot, c + K - by_pool)
                    pe.wait_ge(s_hot_pool, by_pool)
                    pe.wait_ge(s_hi_val, c // K + 1)
                ins = t.matmul(ps_rows, lo_hot[:, c, :], hi_val[:, c, :, :],
                               start=(c == 0), stop=(c == PAIRS - 1))
            ins.then_inc(s_rows, 1)
            pe.wait_ge(s_pos, 1)
            for q in range(1, 4):
                bias2(q)

            pe.wait_ge(s_w1, 16 * (E + 1))
            pe.wait_ge(s_w2, 16 * E)

            def turn_x(slot, uses):
                pe.wait_ge(s_got[slot], 16 * uses)
                for c in range(HC):
                    ins = t.transpose(ps_xT[:, c, :], xg[slot][:, c * HK:(c + 1) * HK], ident[:, :])
                ins.then_inc(s_xT, 1)

            def expert(j):
                return pe.value_load(owner[0:1, bass.ds(j, 1) if not isinstance(j, int) else slice(j, j + 1)],
                                     min_val=0, max_val=E - 1)

            def up(e, part, dst, buf):
                for c in range(HC):
                    rows = HK + (c == HC - 1)
                    ins = t.matmul(dst, xT[0:rows, buf, c, :],
                                   w1_sb[0:rows, bass.ds(e * W1E + (2 * c + part) * I, I)],
                                   start=(c == 0), stop=(c == HC - 1))
                return ins

            def turn_a(j):
                pe.wait_ge(s_a, j + 1)
                wait(pe, s_aTc, j)
                for c in range(IC):
                    ins = t.transpose(ps_aT[:, c, :], act_a[:, c * 128:(c + 1) * 128], ident[:, :])
                ins.then_inc(s_aT, 1)

            def down(e, j):
                pe.wait_ge(s_aTc, j + 1)
                wait(pe, s_yc, j)
                for c in range(IC):
                    ins = t.matmul(ps_y, aT[:, c, :], w2_sb[:, bass.ds(e * W2E + c * H, H)],
                                   start=(c == 0), stop=(c == IC - 1))
                ins.then_inc(s_y, 1)

            def step(gi, c):
                j = UNROLL * gi + c
                first = isinstance(j, int) and j == 0
                last = isinstance(j, int) and j == MT - 1
                e = expert(j)
                pe.wait_ge(s_xTc, j + 1)
                wait(pe, s_gluc, j)
                up(e, 0, ps_glu, c % 2).then_inc(s_glu, 1)
                if not first:
                    if isinstance(j, int) and j == 1:
                        pe.wait_ge(s_b2c, 4)
                    turn_a(j - 1)
                if not last:
                    turn_x((c + 1) % RING, UNROLL // RING * gi + (c + 1) // RING + 1)
                wait(pe, s_linc, j)
                up(e, 1, ps_lin, c % 2).then_inc(s_lin, 1)
                if not first:
                    down(expert(j - 1), j - 1)

            pe.wait_ge(s_b2c, 1)
            turn_x(0, 1)
            slot_steps(pe, step)
            turn_a(MT - 1)
            down(expert(MT - 1), MT - 1)


def kernel(**inputs):
    import numpy as np
    import concourse.bacc as bacc
    from concourse.bass_utils import run_bass_kernel_spmd

    a = {k: np.asarray(v) for k, v in inputs.items()}
    x = a["x"][:, :, :SEQ * PATCH].reshape(TILES, CLIPS // TILES, CHANNELS, SEQ, PATCH)
    x = x.transpose(0, 2, 4, 1, 3).reshape(TILES, FC, FK, TT).transpose(0, 2, 1, 3)
    w1 = a["L0_ffn_mlp1_w"].reshape(E, I, 2, HC, HK).transpose(0, 4, 3, 2, 1).reshape(E, HK, W1E)
    b1 = a["L0_ffn_mlp1_b"].reshape(E, I, 2).transpose(0, 2, 1).reshape(1, E, 2 * I)
    w2 = a["L0_ffn_mlp2_w"].reshape(E, H, IC, 128).transpose(0, 3, 2, 1).reshape(E, 128, W2E)
    w = a["L0_attn_W_qkv"]
    arrays = {
        "x": x,
        "tok_w": a["L0_tok_W"].reshape(H, FC, FK).transpose(2, 1, 0),
        "tok_b": a["L0_tok_b"].reshape(1, H),
        "qkv_w": np.concatenate([w[:, 0:H].T.reshape(HC, HK, H), w[:, H:2 * H].T.reshape(HC, HK, H),
                                 a["L0_attn_b_qkv"][H:2 * H].reshape(HC, HK, 1),
                                 w[:, 2 * H:].reshape(HC, HK, H)], axis=2).transpose(1, 0, 2),
        "qk_b": a["L0_attn_b_qkv"][:2 * H].reshape(4, HK).transpose(1, 0),
        "v_b": a["L0_attn_b_qkv"][2 * H:].reshape(1, H),
        "norm_scale": a["L0_ffn_norm_scale"].reshape(1, H),
        "gate_w": a["L0_ffn_gate_w"].reshape(E, HC, HK).transpose(2, 1, 0),
        "gate_b": a["L0_ffn_gate_b"].reshape(1, E),
        "w1": w1,
        "b1": b1,
        "w2": w2,
        "b2": a["L0_ffn_mlp2_b"],
    }
    arrays = {f"in_{k}": np.ascontiguousarray(v) for k, v in arrays.items()}
    nc = bacc.Bacc("TRN2", target_bir_lowering=False, num_devices=1)
    args = [nc.dram_tensor(k, v.shape, mybir.dt.from_np(v.dtype), kind="ExternalInput").ap()
            for k, v in arrays.items()]
    out = nc.dram_tensor("out", (TOKENS + SLOTS, H), F32, kind="ExternalOutput").ap()
    audio_tower_kernel(nc, *args, out)
    r = run_bass_kernel_spmd(nc, [arrays], core_ids=[0])
    return r.results[0]["out"][:TOKENS].reshape(CLIPS, SEQ, H)
```
